# Optimizing a Trainium2 kernel written in Bass

```python
import numpy as np
import jax
import jax.numpy as jnp

def _softmax(x, axis=-1):
    return jax.nn.softmax(x, axis=axis)

def _gelu(x):
    return jax.nn.gelu(x, approximate=True)

def _silu(x):
    return jax.nn.silu(x)

def _sigmoid(x):
    return jax.nn.sigmoid(x)

def _layernorm(x, axis=-1, eps=1e-05):
    m = jnp.mean(x, axis=axis, keepdims=True)
    v = jnp.var(x, axis=axis, keepdims=True)
    return (x - m) / jnp.sqrt(v + eps)

def _scatter_add(tgt, idx, src, axis=0):
    return tgt.at[idx].add(src)

def _segment_sum(src, seg, n):
    return jax.ops.segment_sum(src, seg, n)
kernel_name = 'mk_adaln_attn_ffn_d1_seqx_r4_e69336'

def setup_inputs(seed: int=0):
    np.random.seed(seed)
    _w = jnp.asarray

    def _rec_inputs():
        import jax
        import jax.numpy as jnp
        _rk = jax.random.key(seed)
        x = -0.0003929 + 0.9999 * jax.random.normal(jax.random.fold_in(_rk, 1), (2, 1024, 256), jnp.float32)
        _lenS = 1024 - jax.random.randint(jax.random.fold_in(_rk, 7), (2,), 0, max(1, 1024 // 4) + 1, jnp.int32)
        _lenS2 = 1024 - jax.random.randint(jax.random.fold_in(_rk, 8), (2,), 0, max(1, 1024 // 4) + 1, jnp.int32)
        cond_1024 = jax.random.uniform(jax.random.fold_in(_rk, 11), (2, 256), jnp.float32, 0.0, 0.999994)
        return (x, cond_1024)
    x, cond_1024 = _rec_inputs()

    def _L0_cond_setup():
        import jax, jax.numpy as jnp
        import numpy as np
        DT = 0.001
        T_SUBSTEPS = 4
        key = jax.random.key(seed)
        k1, k2 = jax.random.split(key)
        inputs = jax.random.normal(k1, (32, 128, 256), dtype=jnp.float32)
        initial_state = jax.random.uniform(k2, (32, 256), dtype=jnp.float32)
        return {'inputs': inputs, 'initial_state': initial_state}
    _L0_cond_all = _L0_cond_setup()
    _L0_cond_in = {k: v for k, v in _L0_cond_all.items() if k in ()}
    del _L0_cond_all

    def _L0_attn_setup():
        import jax, jax.numpy as jnp
        import numpy as np
        B, L, D, H = (2, 512, 256, 4)
        DV = D // H
        P = 5
        CHUNK = 32
        CONV_K = 4
        FIR_K = (3, 15, 64)

        def _dwconv(x, w):
            K = w.shape[1]
            xt = jnp.pad(jnp.transpose(x, (0, 2, 1)), ((0, 0), (0, 0), (K - 1, 0)))
            y = jax.lax.conv_general_dilated(xt, w[:, None, :], (1,), 'VALID', dimension_numbers=('NCH', 'OIH', 'NCH'), feature_group_count=w.shape[0])
            return jnp.transpose(y, (0, 2, 1))

        def _l2norm(x):
            return x * jax.lax.rsqrt(jnp.sum(x * x, -1, keepdims=True) + 1e-06)

        def _delta_rule_chunkwise(q, k, v, beta, chunk=CHUNK):
            b, h, Lp, dk = q.shape
            dv = v.shape[-1]
            n = Lp // chunk
            q = _l2norm(q)
            k = _l2norm(k)
            v = v * beta[..., None]
            kb = k * beta[..., None]
            r = lambda t: t.reshape(b, h, n, chunk, -1)
            q, k, v, kb = (r(q), r(k), r(v), r(kb))
            sw = lambda t: jnp.swapaxes(t, -1, -2)
            strict = jnp.tril(jnp.ones((chunk, chunk), bool), -1)
            attn = jnp.where(strict, -(kb @ sw(k)), 0.0)
            T = jnp.linalg.inv(jnp.eye(chunk, dtype=q.dtype) - attn)
            u = T @ v
            w = T @ kb
            incl = jnp.tril(jnp.ones((chunk, chunk), bool), 0)
            qs, ks, us, ws = (jnp.moveaxis(t, 2, 0) for t in (q, k, u, w))
            S0 = jnp.zeros((b, h, dk, dv), q.dtype)

            def step(S, inp):
                q_i, k_i, u0, w_i = inp
                local = jnp.where(incl, q_i @ sw(k_i), 0.0)
                u_i = u0 - w_i @ S
                o_i = q_i @ S + local @ u_i
                return (S + sw(k_i) @ u_i, o_i)
            S, o = jax.lax.scan(step, S0, (qs, ks, us, ws))
            return (jnp.moveaxis(o, 0, 2).reshape(b, h, Lp, dv), S)

        def _stats(t):
            m = jnp.mean(t, -1, keepdims=True)
            v = jnp.mean(t * t, -1, keepdims=True)
            a = jnp.mean(jnp.abs(t), -1, keepdims=True)
            nrm = jnp.sqrt(jnp.sum(t * t, -1, keepdims=True))
            s = jnp.concatenate([jnp.broadcast_to(x, t.shape) for x in (m, v, a, nrm)], -1)
            return s.reshape(t.shape[0], t.shape[1], -1)

        def _forward(hs, Wq, Wk, Wv, conv_q, conv_k, conv_v, Wb, fir_s, fir_m, fir_l, gW1, gb1, gW2, gb2, log_tau, eps_logit, norm_w, Wo):
            b, Ln, _ = hs.shape
            q = jax.nn.silu(_dwconv(hs @ Wq, conv_q))
            k = jax.nn.silu(_dwconv(hs @ Wk, conv_k))
            v = jax.nn.silu(_dwconv(hs @ Wv, conv_v))
            beta = jax.nn.sigmoid(hs @ Wb)
            bh = lambda t: jnp.transpose(t.reshape(b, Ln, H, -1), (0, 2, 1, 3))
            o_d, _ = _delta_rule_chunkwise(bh(q), bh(k), bh(v), jnp.transpose(beta, (0, 2, 1)))
            delta_path = jnp.transpose(o_d, (0, 2, 1, 3))
            paths = jnp.stack([_dwconv(v, fir_s).reshape(b, Ln, H, DV), _dwconv(v, fir_m).reshape(b, Ln, H, DV), _dwconv(v, fir_l).reshape(b, Ln, H, DV), delta_path, v.reshape(b, Ln, H, DV)], axis=3)
            stats_flat = jnp.concatenate([_stats(paths[..., p, :]) for p in range(P)], -1)
            gate_in = jnp.concatenate([hs, stats_flat], -1)
            logits = jax.nn.gelu(gate_in @ gW1 + gb1, approximate=False) @ gW2 + gb2
            logits = logits.reshape(b, Ln, H, P)
            tau = jax.nn.softplus(log_tau) + 0.5
            probs = jax.nn.softmax(logits / tau[:, None], -1)
            eps = jax.nn.sigmoid(eps_logit) * 0.2
            probs = probs * (1.0 - jnp.sum(eps, -1, keepdims=True)) + eps
            o = jnp.einsum('blhp,blhpd->blhd', probs, paths)
            o = o * jax.lax.rsqrt(jnp.mean(o * o, -1, keepdims=True) + 1e-05) * norm_w
            return o.reshape(b, Ln, D) @ Wo
        key = jax.random.key(seed)
        ks = jax.random.split(key, 14)
        lin = lambda kk, fan_in, shape: jax.random.normal(kk, shape, jnp.float32) / np.float32(np.sqrt(fan_in))

        def fir(kk, K):
            w = np.zeros((D, K), np.float32)
            w[:, -1] = 1.0
            return jnp.asarray(w) + 0.001 * jax.random.normal(kk, (D, K), jnp.float32)
        in_gate = D + 4 * DV * H * P
        HF = 2 * D
        gb2 = np.zeros((H * P,), np.float32)
        gb2[np.arange(H) * P + P - 1] = 1.0
        return {'hidden_states': jax.random.normal(ks[0], (B, L, D), jnp.float32), 'Wq': lin(ks[1], D, (D, D)), 'Wk': lin(ks[2], D, (D, D)), 'Wv': lin(ks[3], D, (D, D)), 'conv_q': lin(ks[4], CONV_K, (D, CONV_K)), 'conv_k': lin(ks[5], CONV_K, (D, CONV_K)), 'conv_v': lin(ks[6], CONV_K, (D, CONV_K)), 'Wb': lin(ks[7], D, (D, H)), 'fir_s': fir(ks[8], FIR_K[0]), 'fir_m': fir(ks[9], FIR_K[1]), 'fir_l': fir(ks[10], FIR_K[2]), 'gW1': lin(ks[11], in_gate, (in_gate, HF)), 'gb1': jnp.zeros((HF,), jnp.float32), 'gW2': lin(ks[12], HF, (HF, H * P)), 'gb2': jnp.asarray(gb2), 'log_tau': jnp.zeros((H,), jnp.float32), 'eps_logit': jnp.zeros((H, P), jnp.float32), 'norm_w': jnp.ones((DV,), jnp.float32), 'Wo': lin(ks[13], D, (D, D))}
    _L0_attn_all = _L0_attn_setup()
    _L0_attn_in = {k: v for k, v in _L0_attn_all.items() if k in ('Wq', 'Wk', 'Wv', 'conv_q', 'conv_k', 'conv_v', 'Wb', 'fir_s', 'fir_m', 'fir_l', 'gW1', 'gb1', 'gW2', 'gb2', 'log_tau', 'eps_logit', 'norm_w', 'Wo')}
    del _L0_attn_all

    def _L0_cond2_setup():
        import jax, jax.numpy as jnp
        import numpy as np
        LATENT = 256
        key = jax.random.key(seed)
        k1, k2, k3, k4 = jax.random.split(key, 4)
        B, T, D = (64, 128, LATENT)
        h_t = jax.random.normal(k1, (B, D), dtype=jnp.float32)
        z = jax.random.normal(k2, (B, T, D), dtype=jnp.float32)
        bound = 1.0 / np.sqrt(2 * D)
        W = jax.random.uniform(k3, (D, 2 * D), minval=-bound, maxval=bound, dtype=jnp.float32)
        b = jax.random.uniform(k4, (D,), minval=-bound, maxval=bound, dtype=jnp.float32)
        alpha = jnp.full((D,), 0.1, dtype=jnp.float32)
        return {'h_t': h_t, 'z': z, 'W': W, 'b': b, 'alpha': alpha}
    _L0_cond2_all = _L0_cond2_setup()
    _L0_cond2_in = {k: v for k, v in _L0_cond2_all.items() if k in ('W', 'b', 'alpha')}
    del _L0_cond2_all

    def _L0_ffn_setup():
        import jax, jax.numpy as jnp
        import numpy as np
        B, S, D, H, E = (4, 512, 256, 1024, 8)
        key = jax.random.key(seed)
        ks = jax.random.split(key, 8)
        s_d = 1.0 / np.sqrt(D)
        s_h = 1.0 / np.sqrt(H)
        return {'x': jax.random.normal(ks[0], (B, S, D), dtype=jnp.float32), 'gate_w': jax.random.uniform(ks[1], (E, D), jnp.float32, -s_d, s_d), 'gate_b': jax.random.uniform(ks[2], (E,), jnp.float32, -s_d, s_d), 'w1': jax.random.uniform(ks[3], (E, H, D), jnp.float32, -s_d, s_d), 'b1': jax.random.uniform(ks[4], (E, H), jnp.float32, -s_d, s_d), 'w2': jax.random.uniform(ks[5], (E, D, H), jnp.float32, -s_h, s_h), 'b2': jax.random.uniform(ks[6], (E, D), jnp.float32, -s_h, s_h)}
    _L0_ffn_all = _L0_ffn_setup()
    _L0_ffn_in = {k: v for k, v in _L0_ffn_all.items() if k in ('gate_w', 'gate_b', 'w1', 'b1', 'w2', 'b2')}
    del _L0_ffn_all
    return {'x': x, 'cond_1024': cond_1024, 'L0_attn_Wq': _L0_attn_in['Wq'], 'L0_attn_Wk': _L0_attn_in['Wk'], 'L0_attn_Wv': _L0_attn_in['Wv'], 'L0_attn_conv_q': _L0_attn_in['conv_q'], 'L0_attn_conv_k': _L0_attn_in['conv_k'], 'L0_attn_conv_v': _L0_attn_in['conv_v'], 'L0_attn_Wb': _L0_attn_in['Wb'], 'L0_attn_fir_s': _L0_attn_in['fir_s'], 'L0_attn_fir_m': _L0_attn_in['fir_m'], 'L0_attn_fir_l': _L0_attn_in['fir_l'], 'L0_attn_gW1': _L0_attn_in['gW1'], 'L0_attn_gb1': _L0_attn_in['gb1'], 'L0_attn_gW2': _L0_attn_in['gW2'], 'L0_attn_gb2': _L0_attn_in['gb2'], 'L0_attn_log_tau': _L0_attn_in['log_tau'], 'L0_attn_eps_logit': _L0_attn_in['eps_logit'], 'L0_attn_norm_w': _L0_attn_in['norm_w'], 'L0_attn_Wo': _L0_attn_in['Wo'], 'L0_cond2_W': _L0_cond2_in['W'], 'L0_cond2_b': _L0_cond2_in['b'], 'L0_cond2_alpha': _L0_cond2_in['alpha'], 'L0_ffn_gate_w': _L0_ffn_in['gate_w'], 'L0_ffn_gate_b': _L0_ffn_in['gate_b'], 'L0_ffn_w1': _L0_ffn_in['w1'], 'L0_ffn_b1': _L0_ffn_in['b1'], 'L0_ffn_w2': _L0_ffn_in['w2'], 'L0_ffn_b2': _L0_ffn_in['b2']}

def reference(x, cond_1024, L0_attn_Wq, L0_attn_Wk, L0_attn_Wv, L0_attn_conv_q, L0_attn_conv_k, L0_attn_conv_v, L0_attn_Wb, L0_attn_fir_s, L0_attn_fir_m, L0_attn_fir_l, L0_attn_gW1, L0_attn_gb1, L0_attn_gW2, L0_attn_gb2, L0_attn_log_tau, L0_attn_eps_logit, L0_attn_norm_w, L0_attn_Wo, L0_cond2_W, L0_cond2_b, L0_cond2_alpha, L0_ffn_gate_w, L0_ffn_gate_b, L0_ffn_w1, L0_ffn_b1, L0_ffn_w2, L0_ffn_b2):
    import jax
    import jax.numpy as jnp

    def _L0_cond_ref(inputs, initial_state):
        import jax, jax.numpy as jnp
        import numpy as np
        DT = 0.001
        T_SUBSTEPS = 4
        rates = jax.nn.relu(inputs) * DT

        def step(voltage, rate_t):
            spikes = voltage
            for _ in range(T_SUBSTEPS):
                voltage = voltage + rate_t
                spikes = jnp.floor(voltage)
                voltage = voltage - spikes
            return (voltage, spikes)
        _, all_spikes = jax.lax.scan(step, initial_state, jnp.swapaxes(rates, 0, 1))
        return jnp.swapaxes(all_spikes, 0, 1) / DT

    def _L0_attn_ref(hidden_states, Wq, Wk, Wv, conv_q, conv_k, conv_v, Wb, fir_s, fir_m, fir_l, gW1, gb1, gW2, gb2, log_tau, eps_logit, norm_w, Wo):
        import jax, jax.numpy as jnp
        import numpy as np
        B, L, D, H = (2, 512, 256, 4)
        DV = D // H
        P = 5
        CHUNK = 32
        CONV_K = 4
        FIR_K = (3, 15, 64)

        def _dwconv(x, w):
            K = w.shape[1]
            xt = jnp.pad(jnp.transpose(x, (0, 2, 1)), ((0, 0), (0, 0), (K - 1, 0)))
            y = jax.lax.conv_general_dilated(xt, w[:, None, :], (1,), 'VALID', dimension_numbers=('NCH', 'OIH', 'NCH'), feature_group_count=w.shape[0])
            return jnp.transpose(y, (0, 2, 1))

        def _l2norm(x):
            return x * jax.lax.rsqrt(jnp.sum(x * x, -1, keepdims=True) + 1e-06)

        def _delta_rule_chunkwise(q, k, v, beta, chunk=CHUNK):
            b, h, Lp, dk = q.shape
            dv = v.shape[-1]
            n = Lp // chunk
            q = _l2norm(q)
            k = _l2norm(k)
            v = v * beta[..., None]
            kb = k * beta[..., None]
            r = lambda t: t.reshape(b, h, n, chunk, -1)
            q, k, v, kb = (r(q), r(k), r(v), r(kb))
            sw = lambda t: jnp.swapaxes(t, -1, -2)
            strict = jnp.tril(jnp.ones((chunk, chunk), bool), -1)
            attn = jnp.where(strict, -(kb @ sw(k)), 0.0)
            T = jnp.linalg.inv(jnp.eye(chunk, dtype=q.dtype) - attn)
            u = T @ v
            w = T @ kb
            incl = jnp.tril(jnp.ones((chunk, chunk), bool), 0)
            qs, ks, us, ws = (jnp.moveaxis(t, 2, 0) for t in (q, k, u, w))
            S0 = jnp.zeros((b, h, dk, dv), q.dtype)

            def step(S, inp):
                q_i, k_i, u0, w_i = inp
                local = jnp.where(incl, q_i @ sw(k_i), 0.0)
                u_i = u0 - w_i @ S
                o_i = q_i @ S + local @ u_i
                return (S + sw(k_i) @ u_i, o_i)
            S, o = jax.lax.scan(step, S0, (qs, ks, us, ws))
            return (jnp.moveaxis(o, 0, 2).reshape(b, h, Lp, dv), S)

        def _stats(t):
            m = jnp.mean(t, -1, keepdims=True)
            v = jnp.mean(t * t, -1, keepdims=True)
            a = jnp.mean(jnp.abs(t), -1, keepdims=True)
            nrm = jnp.sqrt(jnp.sum(t * t, -1, keepdims=True))
            s = jnp.concatenate([jnp.broadcast_to(x, t.shape) for x in (m, v, a, nrm)], -1)
            return s.reshape(t.shape[0], t.shape[1], -1)

        def _forward(hs, Wq, Wk, Wv, conv_q, conv_k, conv_v, Wb, fir_s, fir_m, fir_l, gW1, gb1, gW2, gb2, log_tau, eps_logit, norm_w, Wo):
            b, Ln, _ = hs.shape
            q = jax.nn.silu(_dwconv(hs @ Wq, conv_q))
            k = jax.nn.silu(_dwconv(hs @ Wk, conv_k))
            v = jax.nn.silu(_dwconv(hs @ Wv, conv_v))
            beta = jax.nn.sigmoid(hs @ Wb)
            bh = lambda t: jnp.transpose(t.reshape(b, Ln, H, -1), (0, 2, 1, 3))
            o_d, _ = _delta_rule_chunkwise(bh(q), bh(k), bh(v), jnp.transpose(beta, (0, 2, 1)))
            delta_path = jnp.transpose(o_d, (0, 2, 1, 3))
            paths = jnp.stack([_dwconv(v, fir_s).reshape(b, Ln, H, DV), _dwconv(v, fir_m).reshape(b, Ln, H, DV), _dwconv(v, fir_l).reshape(b, Ln, H, DV), delta_path, v.reshape(b, Ln, H, DV)], axis=3)
            stats_flat = jnp.concatenate([_stats(paths[..., p, :]) for p in range(P)], -1)
            gate_in = jnp.concatenate([hs, stats_flat], -1)
            logits = jax.nn.gelu(gate_in @ gW1 + gb1, approximate=False) @ gW2 + gb2
            logits = logits.reshape(b, Ln, H, P)
            tau = jax.nn.softplus(log_tau) + 0.5
            probs = jax.nn.softmax(logits / tau[:, None], -1)
            eps = jax.nn.sigmoid(eps_logit) * 0.2
            probs = probs * (1.0 - jnp.sum(eps, -1, keepdims=True)) + eps
            o = jnp.einsum('blhp,blhpd->blhd', probs, paths)
            o = o * jax.lax.rsqrt(jnp.mean(o * o, -1, keepdims=True) + 1e-05) * norm_w
            return o.reshape(b, Ln, D) @ Wo
        return _forward(hidden_states, Wq, Wk, Wv, conv_q, conv_k, conv_v, Wb, fir_s, fir_m, fir_l, gW1, gb1, gW2, gb2, log_tau, eps_logit, norm_w, Wo)

    def _L0_cond2_ref(h_t, z, W, b, alpha):
        import jax, jax.numpy as jnp
        import numpy as np
        LATENT = 256
        D = h_t.shape[-1]
        Wh = W[:, :D]
        Wz = W[:, D:]
        leak = 1.0 - alpha

        def step(h, z_t):
            gate = jax.nn.sigmoid(h @ Wh.T + z_t @ Wz.T + b)
            h_new = jnp.tanh(h * leak + gate * z_t)
            return (h_new, h_new)
        _, hs = jax.lax.scan(step, h_t, jnp.swapaxes(z, 0, 1))
        return jnp.swapaxes(hs, 0, 1)

    def _L0_ffn_ref(x, gate_w, gate_b, w1, b1, w2, b2):
        import jax, jax.numpy as jnp
        import numpy as np
        B, S, D, H, E = (4, 512, 256, 1024, 8)
        b, s, d = x.shape
        xf = x.reshape(-1, d)
        logits = xf @ gate_w.T + gate_b
        top1 = jnp.argmax(logits, axis=-1)
        out = jnp.zeros_like(xf)
        n_experts = w1.shape[0]
        for e in range(n_experts):
            h = jax.nn.relu(xf @ w1[e].T + b1[e])
            y = h @ w2[e].T + b2[e]
            out = out + jnp.where((top1 == e)[:, None], y, jnp.zeros((), y.dtype))
        return out.reshape(b, s, d)
    x = x + _L0_attn_ref(_L0_cond_ref(x, cond_1024), L0_attn_Wq, L0_attn_Wk, L0_attn_Wv, L0_attn_conv_q, L0_attn_conv_k, L0_attn_conv_v, L0_attn_Wb, L0_attn_fir_s, L0_attn_fir_m, L0_attn_fir_l, L0_attn_gW1, L0_attn_gb1, L0_attn_gW2, L0_attn_gb2, L0_attn_log_tau, L0_attn_eps_logit, L0_attn_norm_w, L0_attn_Wo)
    x = x + _L0_ffn_ref(_L0_cond2_ref(cond_1024, x, L0_cond2_W, L0_cond2_b, L0_cond2_alpha), L0_ffn_gate_w, L0_ffn_gate_b, L0_ffn_w1, L0_ffn_b1, L0_ffn_w2, L0_ffn_b2)
    return x

_drawn_inputs = setup_inputs


def setup_inputs(seed=0):
    import zlib

    import numpy as np

    out = dict(_drawn_inputs(seed))
    spreads = {'L0_attn_gb1': (0.0, 0.8),
     'L0_attn_log_tau': (0.0, 2.0),
     'L0_attn_eps_logit': (0.0, 0.523),
     'L0_attn_norm_w': (1.0, 0.2),
     'L0_cond2_alpha': (0.10000000149011612, 0.6)}
    factors = {'L0_cond2_b': 7.5, 'L0_ffn_b1': 5.607, 'L0_ffn_b2': 4.416}
    for name, (base, spread) in spreads.items():
        noise = np.random.default_rng([zlib.crc32(name.encode()), seed]).standard_normal(out[name].shape)
        drawn = base * np.exp(spread * noise) if base else spread * noise
        out[name] = jnp.asarray(drawn.astype(out[name].dtype))
    for name, factor in factors.items():
        out[name] = (out[name] * factor).astype(out[name].dtype)
    return out
```

```python
from collections import namedtuple
from contextlib import ExitStack

import numpy as np

import concourse.bass as bass
from concourse import mybir

F32 = mybir.dt.float32
ALU = mybir.AluOpType
ACT = mybir.ActivationFunctionType
AX = mybir.AxisListType

P = 128
B, T, D = 2, 1024, 256
C = D // P
J = C * B
H, DV = 4, 64
NP = 5
NS = 4
SUB = 4
DT = 0.001
PER_DT = float(np.float32(1) / np.float32(DT))
KQ = 4
FIR = (3, 15, 64)
FPAD = max(FIR) - 1
HF = 512
E, EH = 8, 1024
N = 512
SEG = 128
BLOCKS = B * T // P + E - 1
LEVELS = 7


class Shared:
    pass


def load_and_spike(nc, d, m):
    PARTS = 2
    TU = T // PARTS
    SU = TU * SUB
    UNITS = PARTS * J
    RING = J
    HALF = float(1.5 * 2 ** 23)
    with ExitStack() as own:
        sb = lambda n, s: own.enter_context(nc.sbuf_tensor("spike_" + n, s, F32))
        sem = lambda n: m.whole.enter_context(nc.semaphore("spike_" + n))
        v0 = sb("v0", [P, J])
        v_start = sb("v_start", [P, J])
        v_low = sb("v_low", [P, J])
        rate = [sb(f"rate{i}", [P, SU]) for i in range(RING)]
        volt = [sb(f"volt{i}", [P, 1 + SU]) for i in range(RING)]
        spikes = [sb(f"spikes{i}", [P, SU]) for i in range(RING)]
        whole = [sb(f"whole{i}", [P, 1 + SU]) for i in range(RING)]
        bad = sb("bad", [P, 2 * UNITS])
        low = sb("low", [P, 1])
        half = sb("half", [P, 1])
        found = own.enter_context(nc.sbuf_tensor("found", [P, 2], F32))
        found_int = own.enter_context(nc.sbuf_tensor("found_int", [1, 1], mybir.dt.int32))
        pick = sb("pick", [P, 2 * P])
        W_TILES = NS * NP * H * DV // P
        W_CHUNK = 5
        CHUNKS = W_TILES // W_CHUNK
        wbuf = sb("wbuf", [P, 2, W_CHUNK, HF])
        w_bank = own.enter_context(nc.psum_tensor("w_bank", [P, HF], F32))
        bad_sum = own.enter_context(nc.psum_tensor("bad_sum", [P, 2 * UNITS], F32))
        (x_in, edge_set, pick_in, w_used, w_copied, started, rated, scanned1, scanned2, scanned3, rounded, counted,
         flagged, shifted, corrected, checked, bad_added, spiked, joined, exact) = map(sem, (
             "x_in", "edge_set", "pick_in", "w_used", "w_copied", "started", "rated", "scanned1", "scanned2",
             "scanned3", "rounded", "counted", "flagged", "shifted", "corrected", "checked", "bad_added", "spiked",
             "joined", "exact"))
        w_in = [sem(f"gate_w_in{i}") for i in range(2)]
        w_stat = d.gW1[D:, :].rearrange("(k p) n -> p k n", p=P)

        block = own.enter_context(nc.Block())

        @block.sync
        def _(sp):
            for c in range(C):
                sp.dma_start(m.xT[:, c * B:(c + 1) * B, :], d.xT[c * P:(c + 1) * P]).then_inc(x_in, 16)
                sp.dma_start(v0[:, c * B:(c + 1) * B], d.condT[c * P:(c + 1) * P]).then_inc(x_in, 16)
            sp.dma_start(pick[:], d.c_pick).then_inc(pick_in, 16)
            for ch in range(CHUNKS):
                if ch >= 2:
                    sp.wait_ge(w_used, ch - 1)
                sp.dma_start(wbuf[:, ch % 2], w_stat[:, ch * W_CHUNK:(ch + 1) * W_CHUNK, :]).then_inc(w_in[ch % 2], 16)

        @block.gpsimd
        def _(pool):
            for i in range(RING):
                nc.gpsimd.memset(whole[i][:, 0:1], HALF).then_inc(edge_set, 1)
                nc.gpsimd.memset(volt[i][:, 0:1], 0.0).then_inc(edge_set, 1)
            nc.gpsimd.memset(low[:], -(1.0 - 2.0 ** -24)).then_inc(edge_set, 1)
            nc.gpsimd.memset(half[:], HALF).then_inc(edge_set, 1)
            pool.wait_ge(edge_set, 2 * RING + 2)

            def count(u):
                i = u % RING
                pool.wait_ge(rounded, u + 1)
                if u >= RING:
                    pool.wait_ge(spiked, u - RING + 1)
                nc.gpsimd.tensor_tensor(spikes[i][:], whole[i][:, 1:], whole[i][:, :SU], ALU.subtract).then_inc(counted, 1)

            def correct(u):
                i = u % RING
                pool.wait_ge(flagged, 2 * u + 2)
                pool.wait_ge(counted, u + 1)
                nc.gpsimd.tensor_tensor(spikes[i][:], spikes[i][:], volt[i][:, 1:], ALU.subtract).then_inc(shifted, 1)
                pool.wait_ge(shifted, u + 1)
                nc.gpsimd.tensor_tensor(spikes[i][:], spikes[i][:], volt[i][:, :SU], ALU.add).then_inc(corrected, 1)

            for u in range(UNITS + 1):
                if u < UNITS:
                    count(u)
                if u >= 1:
                    correct(u - 1)

        @block.scalar
        def _(act):
            act.wait_ge(edge_set, 2 * RING + 2)

            def round_(u):
                act.wait_ge(scanned1, u + 1)
                nc.scalar.activation(whole[u % RING][:, 1:], volt[u % RING][:, 1:], ACT.Identity,
                                     bias=half[:]).then_inc(rounded, 1)

            def check(u):
                act.wait_ge(scanned3, u + 1)
                i = u % RING
                nc.scalar.activation(whole[i][:, 1:], volt[i][:, 1:], ACT.Relu, scale=-1.0,
                                     accum_out=bad[:, 2 * u:2 * u + 1]).then_inc(checked, 1)
                act.wait_ge(checked, 2 * u + 1)
                nc.scalar.activation(whole[i][:, 1:], volt[i][:, 1:], ACT.Relu, bias=low[:],
                                     accum_out=bad[:, 2 * u + 1:2 * u + 2]).then_inc(checked, 1)
                act.wait_ge(checked, 2 * u + 2)

            for u in range(UNITS + 2):
                if u < UNITS:
                    round_(u)
                if u >= 2:
                    check(u - 2)
            act.wait_ge(w_used, CHUNKS)
            nc.scalar.copy(m.w1s[:], w_bank[:]).then_inc(w_copied, 1)
            act.wait_ge(w_copied, 1)

        @block.tensor
        def _(pe):
            pe.wait_ge(pick_in, 16)
            for ch in range(CHUNKS):
                pe.wait_ge(w_in[ch % 2], 16 * (ch // 2 + 1))
                for i in range(W_CHUNK):
                    pair, a = divmod(ch * W_CHUNK + i, NS // 2)
                    at = P - 64 * a - pair
                    last = nc.tensor.matmul(w_bank[:], pick[:, at:at + P], wbuf[:, ch % 2, i, :],
                                            start=(ch == 0 and i == 0), stop=(ch == CHUNKS - 1 and i == W_CHUNK - 1))
                last.then_inc(w_used, 1)
            pe.wait_ge(checked, 2 * UNITS)
            nc.tensor.matmul(bad_sum[:], m.ones[:], bad[:], start=True, stop=True).then_inc(bad_added, 1)

        @block.vector
        def _(dve):
            dve.wait_ge(x_in, 4 * 16)
            dve.wait_ge(edge_set, 2 * RING + 2)
            nc.vector.tensor_copy(v_start[:], v0[:]).then_inc(started, 1)
            nc.vector.tensor_scalar(v_low[:], v0[:], -0.5, None, ALU.add).then_inc(started, 1)
            dve.wait_ge(started, 2)

            def first_scan(u):
                part, j = divmod(u, J)
                i = u % RING
                if part:
                    dve.wait_ge(spiked, u - RING + 1)
                    dve.wait_ge(checked, 2 * (u - RING) + 2)
                nc.vector.tensor_scalar(rate[i][:].rearrange("p (t s) -> p t s", s=SUB),
                                        m.xT[:, j, part * TU:(part + 1) * TU].unsqueeze(2).broadcast_to([P, TU, SUB]),
                                        0.0, DT, ALU.max, ALU.mult).then_inc(rated, 1)
                dve.wait_ge(rated, u + 1)
                dve.wait_ge(started, 2 * max(1, u - RING + 2))
                nc.vector.tensor_tensor_scan(volt[i][:, 1:], rate[i][:], rate[i][:], v_low[:, j:j + 1],
                                             ALU.add, ALU.bypass).then_inc(scanned1, 1)

            def second_scan(u):
                i, j = u % RING, u % J
                dve.wait_ge(counted, u + 1)
                nc.vector.tensor_tensor_scan(volt[i][:, 1:], rate[i][:], spikes[i][:], v_start[:, j:j + 1],
                                             ALU.add, ALU.subtract).then_inc(scanned2, 1)
                dve.wait_ge(scanned2, u + 1)
                nc.vector.tensor_scalar(whole[i][:, 1:], volt[i][:, 1:], 1.0, None, ALU.is_ge).then_inc(flagged, 1)
                dve.wait_ge(flagged, 2 * u + 1)
                nc.vector.scalar_tensor_tensor(volt[i][:, 1:], volt[i][:, 1:], 0.0, whole[i][:, 1:],
                                               ALU.is_lt, ALU.subtract).then_inc(flagged, 1)

            def third_scan(u):
                part, j = divmod(u, J)
                i = u % RING
                dve.wait_ge(corrected, u + 1)
                nc.vector.tensor_tensor_scan(volt[i][:, 1:], rate[i][:], spikes[i][:], v_start[:, j:j + 1],
                                             ALU.add, ALU.subtract).then_inc(scanned3, 1)
                nc.vector.tensor_scalar(m.hs[:, j, part * TU:(part + 1) * TU],
                                        spikes[i][:].rearrange("p (t s) -> p t s", s=SUB)[:, :, SUB - 1],
                                        PER_DT, None, ALU.mult).then_inc(spiked, 1)
                if part < PARTS - 1:
                    dve.wait_ge(scanned3, u + 1)
                    nc.vector.tensor_copy(v_start[:, j:j + 1], volt[i][:, SU:SU + 1]).then_inc(started, 1)
                    nc.vector.tensor_scalar(v_low[:, j:j + 1], volt[i][:, SU:SU + 1], -0.5, None,
                                            ALU.add).then_inc(started, 1)

            for u in range(UNITS + 2):
                if u < UNITS:
                    first_scan(u)
                if 1 <= u <= UNITS:
                    second_scan(u - 1)
                if u >= 2:
                    third_scan(u - 2)
            dve.wait_ge(bad_added, 1)
            nc.vector.tensor_reduce(found[:, 0:1], bad_sum[:], AX.X, ALU.add).then_inc(joined, 1)
            dve.wait_ge(joined, 1)
            nc.vector.tensor_scalar(found[:, 1:2], found[:, 0:1], 0.0, None, ALU.is_gt).then_inc(joined, 1)
            dve.wait_ge(joined, 2)
            nc.vector.tensor_copy(found_int[:], found[0:1, 1:2]).then_inc(joined, 1)
            dve.wait_ge(joined, 3)
            dve.wait_ge(spiked, UNITS)
            wrong = dve.value_load(found_int[0:1, 0:1])
            u, n, over, s = (volt[0][:, 4 * a:4 * a + J] for a in range(4))
            with dve.If(wrong > 0):
                nc.vector.tensor_copy(volt[0][:, 16:16 + J], v0[:]).then_inc(exact, 1)
                with dve.Fori(0, T) as t:
                    for k in range(SUB):
                        at = t * (6 * SUB + 1) + (6 * k + 1)
                        dve.wait_ge(exact, at)
                        nc.vector.scalar_tensor_tensor(u, m.xT[:, :, bass.ds(t, 1)].rearrange("p j o -> p (j o)"),
                                                       0.0, volt[0][:, 16:16 + J], ALU.max, ALU.bypass).then_inc(exact, 1)
                        dve.wait_ge(exact, at + 1)
                        nc.vector.scalar_tensor_tensor(u, u, DT, volt[0][:, 16:16 + J], ALU.mult, ALU.add).then_inc(exact, 1)
                        dve.wait_ge(exact, at + 2)
                        nc.vector.tensor_scalar(n, u, HALF, HALF, ALU.add, ALU.subtract).then_inc(exact, 1)
                        dve.wait_ge(exact, at + 3)
                        nc.vector.tensor_tensor(over, n, u, ALU.is_gt).then_inc(exact, 1)
                        dve.wait_ge(exact, at + 4)
                        nc.vector.tensor_tensor(s, n, over, ALU.subtract).then_inc(exact, 1)
                        dve.wait_ge(exact, at + 5)
                        nc.vector.tensor_tensor(volt[0][:, 16:16 + J], u, s, ALU.subtract).then_inc(exact, 1)
                    nc.vector.tensor_scalar(m.hs[:, :, bass.ds(t, 1)].rearrange("p j o -> p (j o)"), s, PER_DT, None,
                                            ALU.mult).then_inc(exact, 1)
            dve.wait_ge(joined, 3)


def project(nc, d, m):
    with ExitStack() as own:
        sb = lambda n, s: own.enter_context(nc.sbuf_tensor("proj_" + n, s, F32))
        sem = lambda n: m.whole.enter_context(nc.semaphore("proj_" + n))
        w = sb("wqkv", [P, 3, C, D])
        wc = sb("wconv", [P, 3, C, KQ])
        wb4 = sb("wb4", [P, C, H])
        wb = sb("wb", [P, C, D])
        pre = sb("pre", [P, 2, KQ - 1 + T])
        y = sb("y", [P, 2, T])
        sq = sb("sq", [P, 2, T])
        pick = sb("pick", [P, 2 * P])
        ROWS = 48
        GROUPS = 2 * J * (T // N)
        spread = sb("spread", [ROWS, GROUPS, P])
        nrm = sb("nrm", [ROWS, N])
        rn = sb("rn", [ROWS, N])
        pj = [own.enter_context(nc.psum_tensor(f"pj{i}", [P, T], F32)) for i in range(2)]
        ps = own.enter_context(nc.psum_tensor("ps", [P, N], F32))
        pb = [own.enter_context(nc.psum_tensor(f"pb{i}", [P, N], F32)) for i in range(2)]
        (w_in, wb_ready, padded, proj_ready, pre_ready, conv_step, conv_ready, silu_ready, sq_ready,
         sum_ready, root_ready, rn_ready, spread_psum, unit_ready, beta_psum, beta_ready) = map(sem, (
             "w_in", "wb_ready", "padded", "proj_ready", "pre_ready", "conv_step", "conv_ready", "silu_ready",
             "sq_ready", "sum_ready", "root_ready", "rn_ready", "spread_psum", "unit_ready", "beta_psum",
             "beta_ready"))
        UNITS = [(i, j) for i in range(3) for j in range(J)]
        HALVES = T // N
        NORMED = 2 * J
        LAG = 2
        BETA = [(j, n) for j in range(J) for n in range(HALVES)]
        dst = [lambda j: m.q[:, j, :], lambda j: m.k[:, j, :], lambda j: m.v[:, j, FPAD:]]
        block = own.enter_context(nc.Block())

        @block.sync
        def _(sp):
            for i, (a, cw) in enumerate(((d.Wq, d.conv_q), (d.Wk, d.conv_k), (d.Wv, d.conv_v))):
                sp.dma_start(w[:, i], a.rearrange("(c p) n -> p c n", p=P)).then_inc(w_in, 16)
                sp.dma_start(wc[:, i], cw.rearrange("(c p) n -> p c n", p=P)).then_inc(w_in, 16)
            sp.dma_start(wb4[:], d.Wb.rearrange("(c p) n -> p c n", p=P)).then_inc(w_in, 16)
            sp.dma_start(pick[:], d.c_pick).then_inc(w_in, 16)
            sp.dma_start(spread[:], d.c_spread).then_inc(w_in, 16)

        @block.tensor
        def _(pe):
            pe.wait_ge(w_in, 9 * 16)

            def sums(u):
                pe.wait_ge(sq_ready, u + 1)
                for n in range(HALVES):
                    g = u * HALVES + n
                    last = nc.tensor.matmul(ps[0:ROWS, :], pick[:, P - g:P - g + ROWS], sq[:, u % 2, n * N:(n + 1) * N],
                                            start=(g == 0), stop=(g == GROUPS - 1))
                last.then_inc(sum_ready, 1)

            for u, (i, j) in enumerate(UNITS):
                if u >= 2:
                    pe.wait_ge(pre_ready, u - 1)
                c, b = divmod(j, B)
                for n in range(HALVES):
                    for k in range(C):
                        last = nc.tensor.matmul(pj[u % 2][:, n * N:(n + 1) * N], w[:, i, k, c * P:(c + 1) * P],
                                                m.hs[:, k * B + b, n * N:(n + 1) * N],
                                                start=(k == 0), stop=(k == C - 1))
                last.then_inc(proj_ready, 1)
                if LAG <= u < LAG + NORMED:
                    sums(u - LAG)
            pe.wait_ge(rn_ready, 1)
            for g in range(GROUPS):
                if g >= 2:
                    pe.wait_ge(unit_ready, g - 1)
                nc.tensor.matmul(pb[g % 2][:], spread[:, g, :], rn[:], start=True, stop=True).then_inc(spread_psum, 1)
            pe.wait_ge(wb_ready, 1)
            for u, (j, n) in enumerate(BETA):
                if u < 2:
                    pe.wait_ge(unit_ready, GROUPS - 1 + u)
                else:
                    pe.wait_ge(beta_ready, u - 1)
                c, b = divmod(j, B)
                for k in range(C):
                    last = nc.tensor.matmul(pb[u % 2][:], wb[:, k, c * P:(c + 1) * P],
                                            m.hs[:, k * B + b, n * N:(n + 1) * N], start=(k == 0), stop=(k == C - 1))
                last.then_inc(beta_psum, 1)

        @block.gpsimd
        def _(pool):
            nc.gpsimd.memset(pre[:, :, 0:KQ - 1], 0.0).then_inc(padded, 1)
            nc.gpsimd.memset(m.v[:, :, 0:FPAD], 0.0).then_inc(padded, 1)
            pool.wait_ge(w_in, 9 * 16)
            nc.gpsimd.tensor_copy(wb[:].rearrange("p c (h v) -> p c h v", v=DV),
                                  wb4[:].unsqueeze(3).broadcast_to([P, C, H, DV])).then_inc(wb_ready, 1)
            pool.wait_ge(padded, 2)

        @block.scalar
        def _(act):
            def silu(u):
                i, j = UNITS[u]
                act.wait_ge(conv_ready, u + 1)
                nc.scalar.activation(dst[i](j), y[:, u % 2, :], ACT.Silu).then_inc(silu_ready, 1)
                if u < NORMED:
                    if u >= 2:
                        act.wait_ge(sum_ready, u - 1)
                    act.wait_ge(silu_ready, u + 1)
                    nc.scalar.activation(sq[:, u % 2, :], dst[i](j), ACT.Square).then_inc(sq_ready, 1)

            for u in range(len(UNITS)):
                act.wait_ge(proj_ready, u + 1)
                if u >= 2:
                    act.wait_ge(conv_ready, u - 1)
                nc.scalar.copy(pre[:, u % 2, KQ - 1:], pj[u % 2][:]).then_inc(pre_ready, 1)
                if u:
                    silu(u - 1)
                if u == LAG + NORMED:
                    act.wait_ge(sum_ready, NORMED)
                    nc.scalar.activation(nrm[:], ps[0:ROWS, :], ACT.Sqrt, bias=m.eps6[0:ROWS, :]).then_inc(root_ready, 1)
            silu(len(UNITS) - 1)
            for u, (j, n) in enumerate(BETA):
                act.wait_ge(beta_psum, u + 1)
                nc.scalar.activation(m.beta[:, j, n * N:(n + 1) * N], pb[u % 2][:], ACT.Sigmoid).then_inc(beta_ready, 1)
            act.wait_ge(silu_ready, len(UNITS))
            act.wait_ge(beta_ready, len(BETA))

        @block.vector
        def _(dve):
            dve.wait_ge(w_in, 9 * 16)
            dve.wait_ge(padded, 1)
            for u, (i, j) in enumerate(UNITS):
                c = j // B
                dve.wait_ge(pre_ready, u + 1)
                if u >= 2:
                    dve.wait_ge(silu_ready, u - 1)
                out = y[:, u % 2, :]
                nc.vector.tensor_scalar(out, pre[:, u % 2, 0:T], wc[:, i, c, 0:1], None, ALU.mult).then_inc(conv_step, 1)
                for k in range(1, KQ):
                    dve.wait_ge(conv_step, (KQ - 1) * u + k)
                    nc.vector.scalar_tensor_tensor(out, pre[:, u % 2, k:k + T], wc[:, i, c, k:k + 1], out,
                                                   ALU.mult, ALU.add).then_inc(conv_step if k < KQ - 1 else conv_ready, 1)
                if u == LAG + NORMED:
                    dve.wait_ge(root_ready, 1)
                    nc.vector.reciprocal(rn[:], nrm[:]).then_inc(rn_ready, 1)
            for g in range(GROUPS):
                u, n = divmod(g, HALVES)
                i, j = UNITS[u]
                dve.wait_ge(spread_psum, g + 1)
                x = (m.q, m.k)[i][:, j, n * N:(n + 1) * N]
                nc.vector.tensor_tensor(x, x, pb[g % 2][:], ALU.mult).then_inc(unit_ready, 1)
            dve.wait_ge(unit_ready, GROUPS)


def attend(nc, d, m):
    with ExitStack() as own:
        sb = lambda n, s: own.enter_context(nc.sbuf_tensor("delta_" + n, s, F32))
        sem = lambda n: m.whole.enter_context(nc.semaphore("delta_" + n))
        masks = sb("masks", [P, LEVELS + 3, P])
        taps = sb("taps", [P, C, sum(FIR)])
        zero = sb("zero", [P, P])
        kn, kb, vb, qn = (sb(n, [P, J, SEG]) for n in ("kn", "kb", "vb", "qn"))
        kn_t, kb_t, vb_t = (sb(n, [P, J, P]) for n in ("kn_t", "kb_t", "vb_t"))
        raw_a, raw_l, at, loc, tm, tt, ys, ym = (
            [sb(f"{n}{e}", [P, J, SEG]) for e in range(2)]
            for n in ("raw_a", "raw_l", "at", "loc", "tm", "tt", "ys", "ym"))
        wt = sb("wt", [P, J, SEG])
        us = sb("us", [P, J, P])
        state = sb("state", [P, J, P])
        bank = lambda n: own.enter_context(nc.psum_tensor(n, [P, J, SEG], F32))
        y_bank = [bank(f"y_bank{e}") for e in range(2)]
        t_bank = [bank(f"t_bank{e}") for e in range(2)]
        s_bank, o_bank, u_bank = bank("s_bank"), bank("o_bank"), bank("u_bank")
        x_bank = bank("x_bank")
        (c_in, cleared, staged, q_staged, a_psum, a_copied, a_masked, at_ready, loc_ready, y_psum, y_copied, y_ready,
         t_first, tt_first, t_psum, t_copied, tt_psum, tt_copied, x_psum, x_copied, u_psum, u_ready, s_psum,
         s_ready, o_psum, o_ready, fir_step) = map(sem, (
             "c_in", "cleared", "staged", "q_staged", "a_psum", "a_copied", "a_masked", "at_ready", "loc_ready", "y_psum",
             "y_copied", "y_ready", "t_first", "tt_first", "t_psum", "t_copied", "tt_psum", "tt_copied", "x_psum",
             "x_copied", "u_psum", "u_ready", "s_psum", "s_ready", "o_psum", "o_ready", "fir_step"))
        hd = lambda e: slice(e * DV, (e + 1) * DV)
        mask = lambda i: masks[:, i, :].unsqueeze(1).broadcast_to([P, J, SEG])
        FILL_T, UPPER_NEG, UPPER_IN = LEVELS, LEVELS + 1, LEVELS + 2
        ITERS = T // SEG
        MID = LEVELS - 2
        LAST = LEVELS - 1
        X_USES = 6

        def segments(eng, body):
            body(0, True, False)
            with eng.Fori(1, ITERS - 1) as it:
                body(it, False, False)
            body(ITERS - 1, False, True)
        block = own.enter_context(nc.Block())

        @block.sync
        def _(sp):
            sp.dma_start(masks[:], d.c_masks).then_inc(c_in, 16)
            o = 0
            for f, w in zip(FIR, (d.fir_s, d.fir_m, d.fir_l)):
                sp.dma_start(taps[:, :, o:o + f], w.rearrange("(c p) n -> p c n", p=P)).then_inc(c_in, 16)
                o += f

        @block.gpsimd
        def _(pool):
            def stage_k(it):
                nc.gpsimd.tensor_copy(kn[:], m.k[:, :, bass.ds(it * SEG, SEG)]).then_inc(staged, 1)

            def stage_kb(it):
                now = bass.ds(it * SEG, SEG)
                nc.gpsimd.tensor_tensor(kb[:], m.k[:, :, now], m.beta[:, :, now], ALU.mult).then_inc(staged, 1)

            def stage_vb(it):
                nc.gpsimd.tensor_tensor(vb[:], m.v[:, :, bass.ds(it * SEG + FPAD, SEG)],
                                        m.beta[:, :, bass.ds(it * SEG, SEG)], ALU.mult).then_inc(staged, 1)

            def local(it, e):
                pool.wait_ge(x_copied, it * X_USES + (4 + e))
                nc.gpsimd.tensor_tensor(loc[e][:], raw_l[e][:], mask(UPPER_IN), ALU.mult).then_inc(loc_ready, 1)

            def body(it, first, last):
                for e in range(2):
                    pool.wait_ge(a_copied, it * 2 + (e + 1))
                    nc.gpsimd.tensor_tensor(at[e][:], raw_a[e][:], mask(UPPER_NEG), ALU.mult).then_inc(a_masked, 1)
                    pool.wait_ge(a_masked, it * 2 + (e + 1))
                    nc.gpsimd.tensor_tensor(at[e][:], at[e][:], m.eye[:].unsqueeze(1).broadcast_to([P, J, SEG]),
                                            ALU.add).then_inc(at_ready, 1)
                for e in range(2):
                    pool.wait_ge(y_copied, it * (2 * LEVELS) + (e + 1))
                    nc.gpsimd.tensor_tensor(tm[e][:], ys[e][:], mask(0), ALU.mult).then_inc(t_first, 1)
                for e in range(2):
                    pool.wait_ge(at_ready, it * 2 + (e + 1))
                    nc.gpsimd.tensor_tensor(tt[e][:], at[e][:], mask(FILL_T), ALU.mult).then_inc(tt_first, 1)
                for l in range(1, LEVELS):
                    for e in range(2):
                        pool.wait_ge(y_copied, it * (2 * LEVELS) + (2 * l + e + 1))
                        nc.gpsimd.tensor_tensor(ym[e][:], ys[e][:], mask(l), ALU.mult).then_inc(y_ready, 1)
                    if l == 2 and not last:
                        pool.wait_ge(x_psum, it * X_USES + 1)
                        stage_kb(it + 1)
                    if l == 3 and not last:
                        pool.wait_ge(x_psum, it * X_USES + 2)
                        stage_vb(it + 1)
                    if l == LAST - 1:
                        local(it, 0)
                    if l == LAST:
                        local(it, 1)
                        if not last:
                            stage_k(it + 1)

            nc.gpsimd.memset(zero[:], 0.0).then_inc(cleared, 1)
            nc.gpsimd.memset(state[:, 0:2], 0.0).then_inc(s_ready, 1)
            nc.gpsimd.memset(state[:, 2:4], 0.0).then_inc(s_ready, 1)
            pool.wait_ge(c_in, 4 * 16)
            stage_kb(0)
            stage_vb(0)
            stage_k(0)
            segments(pool, body)

        @block.scalar
        def _(act):
            def x_out(it, i, out, scale=1.0):
                act.wait_ge(x_psum, it * X_USES + (i + 1))
                nc.scalar.mul(out, x_bank[:], scale).then_inc(x_copied, 1)

            def u_out(n):
                act.wait_ge(u_psum, n)
                nc.scalar.copy(us[:], u_bank[:]).then_inc(u_ready, 1)

            def state_out(n):
                act.wait_ge(s_psum, n)
                for e in range(2):
                    nc.scalar.copy(state[hd(e), :, hd(e)], s_bank[hd(e), :, hd(e)]).then_inc(s_ready, 1)

            def o_out(n):
                act.wait_ge(o_psum, n)
                nc.scalar.copy(m.q[:, :, bass.ds(n * SEG - SEG, SEG)], o_bank[:]).then_inc(o_ready, 1)

            def body(it, first, last):
                for e in range(2):
                    act.wait_ge(a_psum, it * 2 + (e + 1))
                    nc.scalar.copy(raw_a[e][:], y_bank[e][:]).then_inc(a_copied, 1)
                if not first:
                    u_out(it)
                for l in range(LEVELS):
                    for e in range(2):
                        act.wait_ge(y_psum, it * (2 * LEVELS) + (2 * l + e + 1))
                        nc.scalar.copy(ys[e][:], y_bank[e][:]).then_inc(y_copied, 1)
                    if l == 0:
                        nc.scalar.copy(qn[:], m.q[:, :, bass.ds(it * SEG, SEG)]).then_inc(q_staged, 1)
                        continue
                    if l > 1:
                        for e in range(2):
                            act.wait_ge(tt_psum, it * (2 * LAST) + (2 * l + e - 3))
                            nc.scalar.copy(tt[e][:], t_bank[e][:]).then_inc(tt_copied, 1)
                    if l == 1 and not first:
                        state_out(it)
                    for e in range(2):
                        if l < LAST:
                            act.wait_ge(t_psum, it * (2 * MID) + (2 * l + e - 1))
                            nc.scalar.copy(tm[e][:], t_bank[e][:]).then_inc(t_copied, 1)
                        else:
                            act.wait_ge(tt_psum, it * (2 * LAST) + (2 * l + e - 1))
                            nc.scalar.copy(tt[e][:], t_bank[e][:]).then_inc(tt_copied, 1)
                    if l == 1 and not first:
                        o_out(it)
                    if l < LAST:
                        x_out(it, l - 1, (kb_t, vb_t, kn_t, raw_l[0], raw_l[1])[l - 1][:])
                x_out(it, LAST - 1, wt[:], -1.0)

            segments(act, body)
            u_out(ITERS)
            state_out(ITERS)
            o_out(ITERS)
            act.wait_ge(o_ready, ITERS)

        @block.tensor
        def _(pe):
            def group(out, lhs, rhs, done):
                for j in range(J):
                    last = nc.tensor.matmul(out[:, j, :], lhs(j), rhs(j), start=(j == 0), stop=(j == J - 1),
                                            skip_group_check=True)
                last.then_inc(done, 1)

            def turn(out, x, done):
                for j in range(J):
                    last = nc.tensor.transpose(out[:, j, :], x[:, j, :], m.eye[:])
                last.then_inc(done, 1)

            def x_fill(it, i):
                if i:
                    pe.wait_ge(x_copied, it * X_USES + i)
                if i < 3:
                    turn(x_bank, (kb, vb, kn)[i], x_psum)
                else:
                    e = i - 3
                    pe.wait_ge(q_staged, it + 1)
                    group(x_bank, lambda j: kn[hd(e), j, :], lambda j: qn[hd(e), j, :], x_psum)

            def chain_u(n):
                pe.wait_ge(x_copied, n * X_USES)
                pe.wait_ge(s_ready, n * 2)
                for j in range(J):
                    last = nc.tensor.matmul(u_bank[:, j, :], wt[:, j, :], state[:, j, :], start=False,
                                            stop=(j == J - 1), skip_group_check=True)
                last.then_inc(u_psum, 1)

            def chain_so(n):
                pe.wait_ge(u_ready, n)
                for j in range(J):
                    nc.tensor.matmul(o_bank[:, j, :], state[:, j, :], m.q[:, j, bass.ds(n * SEG - SEG, SEG)],
                                     start=(j == 0), stop=False, skip_group_check=True)
                for j in range(J):
                    last = nc.tensor.matmul(s_bank[:, j, :], kn_t[:, j, :], us[:, j, :], start=False, stop=True,
                                            skip_group_check=True)
                last.then_inc(s_psum, 1)
                pe.wait_ge(loc_ready, n * 2)
                for j in range(J):
                    for e in range(2):
                        last = nc.tensor.matmul(o_bank[hd(e), j, :], us[:, j, hd(e)], loc[e][:, j, :], start=False,
                                                stop=(j == J - 1), skip_group_check=True)
                last.then_inc(o_psum, 1)

            def body(it, first, last):
                pe.wait_ge(staged, it * 3 + 3)
                for e in range(2):
                    group(y_bank[e], lambda j: kn[hd(e), j, :], lambda j: kb[hd(e), j, :], a_psum)
                if not first:
                    chain_u(it)
                for e in range(2):
                    pe.wait_ge(at_ready, it * 2 + (e + 1))
                    turn(y_bank[e], at[e], y_psum)
                if not first:
                    chain_so(it)
                for l in range(1, LEVELS):
                    for e in range(2):
                        if l == 1:
                            pe.wait_ge(t_first, it * 2 + (e + 1))
                        else:
                            pe.wait_ge(t_copied, it * (2 * MID) + (2 * (l - 1) + e - 1))
                        group(y_bank[e], lambda j: at[e][:, j, :], lambda j: tm[e][:, j, :], y_psum)
                    if l > 1:
                        for e in range(2):
                            turn(t_bank[e], tm[e], tt_psum)
                    for e in range(2):
                        pe.wait_ge(y_ready, it * (2 * LEVELS - 2) + (2 * l + e - 1))
                        if l == 1:
                            pe.wait_ge(tt_first, it * 2 + (e + 1))
                        else:
                            pe.wait_ge(tt_copied, it * (2 * LAST) + (2 * l + e - 3))
                        if l < LAST:
                            group(t_bank[e], lambda j: tt[e][:, j, :], lambda j: ym[e][:, j, :], t_psum)
                        else:
                            group(t_bank[e], lambda j: ym[e][:, j, :], lambda j: tt[e][:, j, :], tt_psum)
                    if l < LAST:
                        x_fill(it, l - 1)
                pe.wait_ge(x_copied, it * X_USES + (X_USES - 1))
                pe.wait_ge(tt_copied, it * (2 * LAST) + 2 * LAST)
                for e in range(2):
                    for j in range(J):
                        last = nc.tensor.matmul(x_bank[hd(e), j, :], kb_t[:, j, hd(e)], tt[e][:, j, :],
                                                start=(j == 0), stop=(j == J - 1), skip_group_check=True)
                last.then_inc(x_psum, 1)
                for j in range(J):
                    for e in range(2):
                        nc.tensor.matmul(u_bank[:, j, hd(e)], tt[e][:, j, :], vb_t[:, j, hd(e)],
                                         start=(j == 0 and e == 0), stop=False, skip_group_check=True)

            pe.wait_ge(cleared, 1)
            for j in range(J):
                nc.tensor.matmul(s_bank[:, j, :], zero[:], zero[:], start=(j == 0), stop=True, skip_group_check=True)
            segments(pe, body)
            chain_u(ITERS)
            chain_so(ITERS)

        @block.vector
        def _(dve):
            dve.wait_ge(c_in, 4 * 16)
            first = 0
            steps = 0
            for f, out in zip(FIR, (m.fir_s, m.fir_m, m.fir_l)):
                off = FPAD + 1 - f
                for j in range(J):
                    nc.vector.tensor_scalar(out[:, j, :], m.v[:, j, off:off + T], taps[:, j // B, first:first + 1],
                                            None, ALU.mult).then_inc(fir_step, 1)
                with dve.Fori(1, f) as k:
                    for j in range(J):
                        dve.wait_ge(fir_step, k * J + (steps + j + 1 - J))
                        nc.vector.scalar_tensor_tensor(
                            out[:, j, :], m.v[:, j, bass.ds(k + off, T)], taps[:, j // B, bass.ds(k + first, 1)],
                            out[:, j, :], ALU.mult, ALU.add).then_inc(fir_step, 1)
                first += f
                steps += f * J
            dve.wait_ge(fir_step, steps)


def mix(nc, d, m):
    TILES = N // P
    CHUNKS = B * T // N
    PH = NP * H
    with ExitStack() as own:
        sb = lambda n, s: own.enter_context(nc.sbuf_tensor("mix_" + n, s, F32))
        sem = lambda n: m.whole.enter_context(nc.semaphore("mix_" + n))
        path = [sb(f"path{i}", [P, TILES, NP, D]) for i in range(2)]
        sq = sb("path_sq", [P, 2, NP, D])
        st = [sb(f"st{i}", [P, TILES, P]) for i in range(2)]
        st_t = sb("st_t", [P, N])
        gel = sb("gel", [P, HF // P, N])
        w1h = sb("w1h", [P, C, HF])
        w2 = sb("gw2", [P, HF // P, PH])
        wo = sb("wo", [P, C, D])
        nw = sb("nw", [P, 1])
        b2 = sb("gb2r", [P, PH])
        raw = sb("raw", [P, 2, PH])
        itau = sb("itau", [P, PH])
        eps = sb("eps", [P, PH])
        keep = sb("keep", [P, PH])
        tmp = sb("tmp", [P, 4, PH])
        lg = sb("lg", [P, TILES, H, NP])
        top = sb("top", [P, TILES * H])
        pr = [sb(f"pr{i}", [P, TILES, H, NP]) for i in range(2)]
        o = sb("o", [P, TILES, D])
        o2 = sb("o2", [P, TILES, D])
        ms = sb("ms", [P, TILES * H])
        rs = sb("rs", [P, TILES * H])
        o_t = sb("o_t", [P, C, N])
        tok_bank = own.enter_context(nc.psum_tensor("tok_bank", [P, 6, D], F32))
        st_bank = own.enter_context(nc.psum_tensor("st_bank", [P, N], F32))
        hid_bank = [own.enter_context(nc.psum_tensor(f"hid_bank{i}", [P, N], F32)) for i in range(2)]
        wo_bank = [own.enter_context(nc.psum_tensor(f"wo_bank{i}", [P, N], F32)) for i in range(C)]
        names = ("g_in", "w1s_scaled", "gb1_in", "st_set", "small", "soft_exp", "tok_psum", "path_ready", "sq_ready",
                 "plain_sums", "sq_sums", "norm_ready", "st_psum", "st_ready", "hid_psum", "gelu_ready", "lg_psum",
                 "soft", "shifted", "exp_ready", "probs_ready", "weighted", "mixed", "squared", "ms_ready", "root_ready", "rs_ready",
                 "on_ready", "ot_psum", "ot_ready", "wo_psum", "z_ready")
        s = namedtuple("MixSemaphores", names)(*(sem("m_" + n) for n in names))
        srcs = [m.fir_s, m.fir_m, m.fir_l, m.q, m.v]
        where = lambda n: (n // (T // N), (n % (T // N)) * N)
        block = own.enter_context(nc.Block())
        LOADS = 8

        @block.sync
        def _(sp):
            sp.dma_start(w1h[:], d.gW1[0:D, :].rearrange("(c p) n -> p c n", p=P)).then_inc(s.g_in, 16)
            sp.dma_start(w2[:], d.gW2.rearrange("(f p) n -> p f n", p=P)).then_inc(s.g_in, 16)
            sp.dma_start(wo[:], d.Wo.rearrange("(c p) n -> p c n", p=P)).then_inc(s.g_in, 16)
            for h in range(P // DV):
                sp.dma_start(nw[h * DV:(h + 1) * DV, :], d.norm_w.unsqueeze(1)).then_inc(s.g_in, 16)
            sp.dma_start(b2[:], d.gb2.partition_broadcast(P)).then_inc(s.g_in, 16)
            sp.dma_start(raw[:, 0, 0:H], d.log_tau.partition_broadcast(P)).then_inc(s.g_in, 16)
            sp.dma_start(raw[:, 1, :], d.eps_logit.rearrange("h p -> (h p)").partition_broadcast(P)).then_inc(s.g_in, 16)
            sp.wait_ge(s.w1s_scaled, 1)
            sp.dma_start(m.w1s[31:32, :], d.gb1.unsqueeze(0)).then_inc(s.gb1_in, 16)

        @block.gpsimd
        def _(pool):
            for i in range(2):
                nc.gpsimd.memset(st[i][:], 0.0).then_inc(s.st_set, 1)
            pool.wait_ge(s.st_set, 2)
            for i in range(2):
                nc.gpsimd.memset(st[i][:, :, 31:32], 1.0).then_inc(s.st_set, 1)

            def weigh(a):
                n, k = divmod(a, TILES)
                x = path[n % 2][:, k].rearrange("q p (h v) -> q p h v", v=DV)
                w = pr[n % 2][:, k].rearrange("q h p -> q p h").unsqueeze(3).broadcast_to([P, NP, H, DV])
                pool.wait_ge(s.probs_ready, n + 1)
                nc.gpsimd.tensor_tensor(x, x, w, ALU.mult).then_inc(s.weighted, 1)

            for a in range(CHUNKS * TILES):
                weigh(a)

        @block.scalar
        def _(act):
            act.wait_ge(s.small, 2)
            nc.scalar.activation(tmp[:, 1, 0:H], tmp[:, 0, 0:H], ACT.Exp, scale=-1.0).then_inc(s.soft_exp, 1)
            act.wait_ge(s.soft_exp, 1)
            nc.scalar.activation(tmp[:, 2, 0:H], tmp[:, 1, 0:H], ACT.Ln, bias=m.ones[:, 0:1]).then_inc(s.soft_exp, 1)
            act.wait_ge(s.g_in, LOADS * 16)
            nc.scalar.activation(tmp[:, 3, :], raw[:, 1, :], ACT.Sigmoid).then_inc(s.soft_exp, 1)

            def turn(a):
                n, k = divmod(a, TILES)
                act.wait_ge(s.tok_psum, a + 1)
                if n >= 2:
                    act.wait_ge(s.mixed, a - 2 * TILES + 1)
                nc.scalar.copy(path[n % 2][:, k], tok_bank[:, 0:NP]).then_inc(s.path_ready, 1)
                if a >= 2:
                    act.wait_ge(s.sq_sums, a - 1)
                nc.scalar.activation(sq[:, a % 2], tok_bank[:, 0:NP], ACT.Square).then_inc(s.sq_ready, 1)

            def gelu(n):
                act.wait_ge(s.st_psum, n + 1)
                nc.scalar.copy(st_t[:], st_bank[:]).then_inc(s.st_ready, 1)
                for f in range(HF // P):
                    act.wait_ge(s.hid_psum, 4 * n + f + 1)
                    nc.scalar.activation(gel[:, f, :], hid_bank[f % 2][:], ACT.Gelu).then_inc(s.gelu_ready, 1)

            def expo(n):
                act.wait_ge(s.shifted, 2 * n + 1)
                nc.scalar.activation(lg[:], lg[:], ACT.Exp).then_inc(s.exp_ready, 1)

            def norm(n):
                act.wait_ge(s.sq_sums, TILES * (n + 1))
                nc.scalar.activation(st[n % 2][:, :, 96:96 + PH], st[n % 2][:, :, 32:32 + PH], ACT.Sqrt,
                                     bias=m.tiny[:]).then_inc(s.norm_ready, 1)

            def root(n):
                act.wait_ge(s.ms_ready, n + 1)
                nc.scalar.activation(rs[:], ms[:], ACT.Sqrt, bias=m.eps5[:], scale=1.0 / DV).then_inc(s.root_ready, 1)

            def turned_back(a):
                act.wait_ge(s.ot_psum, a + 1)
                k = a % TILES
                nc.scalar.copy(o_t[:, :, k * P:(k + 1) * P],
                               hid_bank[k % 2][:, 0:D].rearrange("p (c t) -> p c t", c=C)).then_inc(s.ot_ready, 1)

            for i in range(CHUNKS + 1):
                for k in range(TILES):
                    if i < CHUNKS:
                        turn(i * TILES + k)
                    if i and k == 1:
                        gelu(i - 1)
                    if i and k == 3:
                        expo(i - 1)
                if i:
                    root(i - 1)
                if i < CHUNKS:
                    norm(i)
                if i:
                    for k in range(TILES):
                        turned_back((i - 1) * TILES + k)

        @block.tensor
        def _(pe):
            def turn(a):
                n, k = divmod(a, TILES)
                b, t0 = where(n)
                if a:
                    pe.wait_ge(s.sq_ready, a)
                for p, x in enumerate(srcs):
                    off = FPAD if x is m.v else 0
                    for c in range(C):
                        last = nc.tensor.transpose(tok_bank[:, p, c * P:(c + 1) * P],
                                                   x[:, c * B + b, off + t0 + k * P:off + t0 + (k + 1) * P], m.eye[:])
                last.then_inc(s.tok_psum, 1)

            def hidden(n):
                b, t0 = where(n)
                pe.wait_ge(s.norm_ready, n + 1)
                pe.wait_ge(s.plain_sums, TILES * (n + 1))
                for k in range(TILES):
                    last = nc.tensor.transpose(st_bank[:, k * P:(k + 1) * P], st[n % 2][:, k, :], m.eye[:])
                last.then_inc(s.st_psum, 1)
                for f in range(HF // P):
                    if n or f >= 2:
                        pe.wait_ge(s.gelu_ready, 4 * n + f - 1)
                    for c in range(C):
                        nc.tensor.matmul(hid_bank[f % 2][:], w1h[:, c, f * P:(f + 1) * P],
                                         m.hs[:, c * B + b, t0:t0 + N], start=(c == 0), stop=False)
                    pe.wait_ge(s.st_ready, n + 1)
                    nc.tensor.matmul(hid_bank[f % 2][:], m.w1s[:, f * P:(f + 1) * P], st_t[:],
                                     start=False, stop=True).then_inc(s.hid_psum, 1)

            def logits(n):
                pe.wait_ge(s.gelu_ready, 4 * n + 4)
                for k in range(TILES):
                    for f in range(HF // P):
                        last = nc.tensor.matmul(st_bank[:, k * PH:(k + 1) * PH], gel[:, f, k * P:(k + 1) * P], w2[:, f, :],
                                                start=(f == 0), stop=(f == HF // P - 1))
                last.then_inc(s.lg_psum, 1)

            def turn_back(a):
                k = a % TILES
                pe.wait_ge(s.on_ready, a // TILES + 1)
                if a >= 2:
                    pe.wait_ge(s.ot_ready, a - 1)
                for c in range(C):
                    last = nc.tensor.transpose(hid_bank[k % 2][:, c * P:(c + 1) * P], o[:, k, c * P:(c + 1) * P],
                                               m.eye[:])
                last.then_inc(s.ot_psum, 1)

            def out_proj(n):
                pe.wait_ge(s.ot_ready, TILES * (n + 1))
                for c in range(C):
                    if n:
                        pe.wait_ge(s.z_ready, C * (n - 1) + c + 1)
                    for k in range(C):
                        last = nc.tensor.matmul(wo_bank[c][:], wo[:, k, c * P:(c + 1) * P], o_t[:, k, :],
                                                start=(k == 0), stop=(k == C - 1))
                    last.then_inc(s.wo_psum, 1)

            pe.wait_ge(s.g_in, LOADS * 16)
            pe.wait_ge(s.st_set, 4)
            pe.wait_ge(s.gb1_in, 16)
            pe.wait_ge(s.w1s_scaled, 2)
            for i in range(CHUNKS + 1):
                for k in range(TILES):
                    if i < CHUNKS:
                        turn(i * TILES + k)
                    if i and k == 1:
                        hidden(i - 1)
                    if i and k == 2:
                        logits(i - 1)
                if i:
                    for k in range(TILES):
                        turn_back((i - 1) * TILES + k)
                    out_proj(i - 1)

        @block.vector
        def _(dve):
            dve.wait_ge(s.g_in, LOADS * 16)
            nc.vector.tensor_scalar(m.w1s[0:96, :], m.w1s[0:96, :], 1.0 / DV, None, ALU.mult).then_inc(s.w1s_scaled, 1)
            nc.vector.tensor_scalar(wo[:].rearrange("p c n -> p (c n)"), wo[:].rearrange("p c n -> p (c n)"),
                                    nw[:], None, ALU.mult).then_inc(s.w1s_scaled, 1)
            nc.vector.tensor_scalar(tmp[:, 1, 0:H], raw[:, 0, 0:H], -1.0, None, ALU.mult).then_inc(s.small, 1)
            dve.wait_ge(s.small, 1)
            nc.vector.tensor_tensor(tmp[:, 0, 0:H], tmp[:, 1, 0:H], raw[:, 0, 0:H], ALU.max).then_inc(s.small, 1)
            dve.wait_ge(s.soft_exp, 2)
            nc.vector.scalar_tensor_tensor(raw[:, 0, 0:H], raw[:, 0, 0:H], 0.0, tmp[:, 2, 0:H], ALU.max,
                                           ALU.add).then_inc(s.small, 1)
            dve.wait_ge(s.small, 3)
            nc.vector.tensor_scalar(raw[:, 0, 0:H], raw[:, 0, 0:H], 0.5, None, ALU.add).then_inc(s.small, 1)
            dve.wait_ge(s.small, 4)
            nc.vector.reciprocal(tmp[:, 0, 0:H], raw[:, 0, 0:H]).then_inc(s.small, 1)
            dve.wait_ge(s.small, 5)
            by_head = lambda x: x.rearrange("p (h q) -> p h q", q=NP)
            nc.vector.tensor_copy(by_head(itau[:]), tmp[:, 0, 0:H].unsqueeze(2).broadcast_to([P, H, NP])).then_inc(s.small, 1)
            dve.wait_ge(s.soft_exp, 3)
            nc.vector.tensor_scalar(eps[:], tmp[:, 3, :], 0.2, None, ALU.mult).then_inc(s.small, 1)
            dve.wait_ge(s.small, 7)
            nc.vector.tensor_reduce(tmp[:, 1, 0:H], by_head(eps[:]), AX.X, ALU.add).then_inc(s.small, 1)
            dve.wait_ge(s.small, 8)
            nc.vector.tensor_scalar(tmp[:, 2, 0:H], tmp[:, 1, 0:H], -1.0, 1.0, ALU.mult, ALU.add).then_inc(s.small, 1)
            dve.wait_ge(s.small, 9)
            nc.vector.tensor_copy(by_head(keep[:]), tmp[:, 2, 0:H].unsqueeze(2).broadcast_to([P, H, NP])).then_inc(s.small, 1)
            dve.wait_ge(s.small, 10)
            dve.wait_ge(s.st_set, 4)

            def sums(a):
                n, k = divmod(a, TILES)
                x = path[n % 2][:, k].rearrange("q p (h v) -> q (p h) v", v=DV)
                dve.wait_ge(s.path_ready, a + 1)
                nc.vector.tensor_reduce(st[n % 2][:, k, 0:PH], x, AX.X, ALU.add)
                nc.vector.tensor_reduce(st[n % 2][:, k, 64:64 + PH], x, AX.X, ALU.add,
                                        apply_absolute_value=True).then_inc(s.plain_sums, 1)
                dve.wait_ge(s.sq_ready, a + 1)
                nc.vector.tensor_reduce(st[n % 2][:, k, 32:32 + PH],
                                        sq[:, a % 2].rearrange("q p (h v) -> q (p h) v", v=DV), AX.X,
                                        ALU.add).then_inc(s.sq_sums, 1)

            SOFT = 6

            def scores(n):
                rows = lambda x: x[:].rearrange("q t h p -> q t (h p)")
                each = lambda x: x[:].unsqueeze(1).broadcast_to([P, TILES, PH])
                flat = lg[:].rearrange("q t h p -> q (t h) p")
                dve.wait_ge(s.lg_psum, n + 1)
                nc.vector.tensor_tensor(rows(lg), st_bank[:, 0:TILES * PH].rearrange("p (t n) -> p t n", t=TILES),
                                        each(b2), ALU.add).then_inc(s.soft, 1)
                dve.wait_ge(s.soft, SOFT * n + 1)
                nc.vector.tensor_tensor(rows(lg), rows(lg), each(itau), ALU.mult).then_inc(s.soft, 1)
                dve.wait_ge(s.soft, SOFT * n + 2)
                nc.vector.tensor_reduce(top[:], flat, AX.X, ALU.max).then_inc(s.soft, 1)
                dve.wait_ge(s.soft, SOFT * n + 3)
                nc.vector.tensor_tensor(flat, flat, top[:].unsqueeze(2).broadcast_to([P, TILES * H, NP]),
                                        ALU.subtract).then_inc(s.shifted, 1)

            def probs(n):
                rows = lambda x: x[:].rearrange("q t h p -> q t (h p)")
                each = lambda x: x[:].unsqueeze(1).broadcast_to([P, TILES, PH])
                flat = lambda x: x[:].rearrange("q t h p -> q (t h) p")
                dve.wait_ge(s.exp_ready, n + 1)
                nc.vector.tensor_reduce(top[:], flat(lg), AX.X, ALU.add).then_inc(s.soft, 1)
                dve.wait_ge(s.soft, SOFT * n + 4)
                nc.vector.reciprocal(top[:], top[:]).then_inc(s.soft, 1)
                dve.wait_ge(s.soft, SOFT * n + 5)
                nc.vector.tensor_tensor(flat(lg), flat(lg), top[:].unsqueeze(2).broadcast_to([P, TILES * H, NP]),
                                        ALU.mult).then_inc(s.soft, 1)
                dve.wait_ge(s.soft, SOFT * n + 6)
                nc.vector.tensor_tensor(rows(lg), rows(lg), each(keep), ALU.mult).then_inc(s.shifted, 1)
                dve.wait_ge(s.shifted, 2 * n + 2)
                nc.vector.tensor_tensor(rows(pr[n % 2]), rows(lg), each(eps), ALU.add).then_inc(s.probs_ready, 1)

            def combine(a):
                n, k = divmod(a, TILES)
                dve.wait_ge(s.weighted, a + 1)
                if n:
                    dve.wait_ge(s.ot_psum, TILES * n)
                nc.vector.tensor_reduce(o[:, k, :], path[n % 2][:, k].rearrange("q p c -> q c p"), AX.X,
                                        ALU.add).then_inc(s.mixed, 1)

            def squares(n):
                dve.wait_ge(s.mixed, TILES * (n + 1))
                nc.vector.tensor_tensor(o2[:], o[:], o[:], ALU.mult).then_inc(s.squared, 1)
                dve.wait_ge(s.squared, n + 1)
                nc.vector.tensor_reduce(ms[:], o2[:].rearrange("q t (h v) -> q (t h) v", v=DV), AX.X,
                                        ALU.add).then_inc(s.ms_ready, 1)

            def normed(n):
                dve.wait_ge(s.root_ready, n + 1)
                nc.vector.reciprocal(rs[:], rs[:]).then_inc(s.rs_ready, 1)
                dve.wait_ge(s.rs_ready, n + 1)
                x = o[:].rearrange("q t (h v) -> q (t h) v", v=DV)
                nc.vector.tensor_tensor(x, x, rs[:].unsqueeze(2).broadcast_to([P, TILES * H, DV]),
                                        ALU.mult).then_inc(s.on_ready, 1)

            def residual(n):
                b, t0 = where(n)
                for c in range(C):
                    x = m.xT[:, c * B + b, t0:t0 + N]
                    dve.wait_ge(s.wo_psum, C * n + c + 1)
                    nc.vector.tensor_tensor(x, x, wo_bank[c][:], ALU.add).then_inc(s.z_ready, 1)

            for i in range(CHUNKS + 1):
                for k in range(TILES):
                    if i < CHUNKS:
                        sums(i * TILES + k)
                    if i and k == 2:
                        scores(i - 1)
                    if i and k == 3:
                        probs(i - 1)
                if i:
                    for k in range(TILES):
                        combine((i - 1) * TILES + k)
                    squares(i - 1)
                    normed(i - 1)
                    residual(i - 1)
            dve.wait_ge(s.z_ready, C * CHUNKS)


def recur(nc, d, m):
    SWEEPS, TOL = 8, 4e-6
    HALVES = T // N
    UNITS = B * HALVES * C
    BODY = 2 * UNITS
    with ExitStack() as own:
        sb = lambda n, s: own.enter_context(nc.sbuf_tensor("recur_" + n, s, F32))
        sem = lambda n: m.whole.enter_context(nc.semaphore("recur_" + n))
        wg = sb("wg", [P, 2 * C, D])
        bias = sb("bias_g", [P, C])
        alpha = sb("alpha", [P, C])
        leak = sb("leak", [P, C])
        leak_neg = sb("leak_neg", [P, C])
        leak_j = sb("leak_j", [P, J])
        zw = sb("zw", [P, J, T])
        other = sb("h_other", [P, J, 1 + T])
        gate = sb("gate", [P, UNITS, N])
        step = sb("step", [P, UNITS, N])
        slope = sb("slope", [P, UNITS, N])
        rest = sb("rest", [P, UNITS, N])
        worst = sb("worst", [P, UNITS])
        fine = sb("fine", [P, UNITS])
        found = sb("found5", [P, 2])
        one = sb("one_step", [P, 3, J])
        start = sb("h_start", [P, C, B])
        zero = sb("zero_row", [P, D])
        found_int = own.enter_context(nc.sbuf_tensor("found5_int", [1, 1], mybir.dt.int32))
        bank = [own.enter_context(nc.psum_tensor(f"r_bank{i}", [P, N], F32)) for i in range(8)]
        names = ("w_in", "ahead", "leaks", "zw_psum", "zw_ready", "h_ready", "a_psum", "g_ready", "gz_ready",
                 "u_ready", "f_ready", "sq_ready", "j_ready", "jp_ready", "c_ready", "diff_ready", "worst_ready",
                 "fine_ready", "fine_psum", "verdict", "seq_h", "seq_psum", "seq_a", "seq_g", "seq_u", "seq_hl")
        s = namedtuple("RecurSemaphores", names)(*(sem(n) for n in names))
        state = (m.h, other)

        def unit(u):
            bn, c = divmod(u % UNITS, C)
            b, n = divmod(bn, HALVES)
            return b, n * N, c

        def before(u):
            b, t0, c = unit(u)
            return state[u // UNITS % 2][:, c * B + b, t0:t0 + N]

        BODIES = SWEEPS * UNITS // BODY
        LAG_U, LAG_J, LAG_REST, LAG_SCAN = 2, 3, 4, 5

        def slots(eng, body, tail):
            for r in range(BODY):
                body(0, r, True)
            with eng.Fori(1, BODIES) as i:
                for r in range(BODY):
                    body(i * BODY, r, False)
            tail(BODIES * BODY)

        block = own.enter_context(nc.Block())

        @block.sync
        def _(sp):
            sp.dma_start(wg[:], d.wgT.rearrange("(k p) n -> p k n", p=P)).then_inc(s.w_in, 16)
            sp.dma_start(bias[:], d.bg).then_inc(s.w_in, 16)
            sp.dma_start(alpha[:], d.alpha).then_inc(s.w_in, 16)
            sp.dma_start(start[:], d.condT.rearrange("(c p) b -> p c b", p=P)).then_inc(s.w_in, 16)
            for e in range(E):
                sp.dma_start(m.w1[:, e], d.w1T[e].rearrange("(c p) n -> p c n", p=P)).then_inc(s.ahead, 16)
            sp.wait_ge(s.leaks, 1)
            sp.dma_start(m.slots_in.rearrange("(k p) n -> p k n", p=P),
                         zero[:].unsqueeze(1).broadcast_to([P, BLOCKS, D])).then_inc(s.ahead, 16)
            sp.wait_ge(s.ahead, 16 * (E + 1))

        W_IN = 16 * 4

        @block.tensor
        def _(pe):
            pe.wait_ge(s.w_in, W_IN)
            for u in range(UNITS):
                b, t0, c = unit(u)
                for k in range(C):
                    last = nc.tensor.matmul(bank[u][:], wg[:, C + k, c * P:(c + 1) * P], m.xT[:, k * B + b, t0:t0 + N],
                                            start=(k == 0), stop=(k == C - 1))
                last.then_inc(s.zw_psum, 1)

            def product(base, u, have):
                b, t0, c = unit(u)
                pe.wait_ge(s.h_ready, base + (u + have))
                for k in range(C):
                    nc.tensor.matmul(bank[u % UNITS][:], wg[:, k, c * P:(c + 1) * P],
                                     state[u // UNITS % 2][:, k * B + b, t0:t0 + N], start=(k == 0), stop=False)
                nc.tensor.matmul(bank[u % UNITS][:], m.eye[:], zw[:, c * B + b, t0:t0 + N],
                                 start=False, stop=True).then_inc(s.a_psum, 1)

            pe.wait_ge(s.zw_ready, UNITS)
            pe.wait_ge(s.leaks, 6)
            slots(pe, lambda base, r, first: product(base, r, C - r % C),
                  lambda base: [product(base, r, C - r % C) for r in range(UNITS)])
            pe.wait_ge(s.fine_ready, 1)
            nc.tensor.matmul(bank[0][:, 0:UNITS], m.ones[:], fine[:], start=True, stop=True).then_inc(s.fine_psum, 1)
            pe.wait_ge(s.verdict, 3)
            apart = pe.value_load(found_int[0:1, 0:1], min_val=0, max_val=1)
            with pe.If(apart > 0):
                with pe.Fori(0, T) as t:
                    pe.wait_ge(s.seq_h, t + 1)
                    for c in range(C):
                        for k in range(C):
                            last = nc.tensor.matmul(bank[0][:, c * B:(c + 1) * B], wg[:, k, c * P:(c + 1) * P],
                                                    m.h[:, k * B:(k + 1) * B, bass.ds(t, 1)].rearrange("p b o -> p (b o)"),
                                                    start=(c == 0 and k == 0), stop=(k == C - 1), skip_group_check=True)
                    last.then_inc(s.seq_psum, 1)
            pe.wait_ge(s.verdict, 3)

        @block.scalar
        def _(act):
            act.wait_ge(s.w_in, W_IN)
            for u in range(UNITS):
                b, t0, c = unit(u)
                j = c * B + b
                nc.scalar.activation(m.h[:, j, 1 + t0:1 + t0 + N], m.xT[:, j, t0:t0 + N], ACT.Tanh,
                                     scale=0.5).then_inc(s.h_ready, 1)
            for u in range(UNITS):
                b, t0, c = unit(u)
                act.wait_ge(s.zw_psum, u + 1)
                nc.scalar.activation(zw[:, c * B + b, t0:t0 + N], bank[u][:], ACT.Identity,
                                     bias=bias[:, c:c + 1]).then_inc(s.zw_ready, 1)

            def sigmoid(base, r):
                act.wait_ge(s.a_psum, base + (r + 1))
                nc.scalar.activation(gate[:, r % UNITS, :], bank[r % UNITS][:], ACT.Sigmoid).then_inc(s.g_ready, 1)

            def tanh(base, r, square=True):
                act.wait_ge(s.u_ready, base + (r + 1))
                nc.scalar.activation(step[:, r % UNITS, :], gate[:, r % UNITS, :], ACT.Tanh).then_inc(s.f_ready, 1)
                if square:
                    act.wait_ge(s.f_ready, base + (r + 1))
                    nc.scalar.activation(slope[:, r % UNITS, :], step[:, r % UNITS, :], ACT.Square).then_inc(s.sq_ready, 1)

            def body(base, r, first):
                if not first or r >= LAG_U:
                    tanh(base, r - LAG_U)
                sigmoid(base, r)

            def tail(base):
                for r in range(UNITS + LAG_U):
                    tanh(base, r - LAG_U, r < LAG_U)
                    if r < UNITS:
                        sigmoid(base, r)

            slots(act, body, tail)
            act.wait_ge(s.verdict, 3)
            apart = act.value_load(found_int[0:1, 0:1], min_val=0, max_val=1)
            with act.If(apart > 0):
                with act.Fori(0, T) as t:
                    act.wait_ge(s.seq_a, t + 1)
                    nc.scalar.activation(one[:, 1, :], one[:, 0, :], ACT.Sigmoid).then_inc(s.seq_g, 1)
                    act.wait_ge(s.seq_u, 2 * t + 2)
                    nc.scalar.activation(m.h[:, :, bass.ds(t + 1, 1)].rearrange("p j o -> p (j o)"), one[:, 2, :],
                                         ACT.Tanh).then_inc(s.seq_h, 1)
            act.wait_ge(s.verdict, 3)

        @block.gpsimd
        def _(pool):
            def weigh(base, r):
                b, t0, c = unit(r)
                pool.wait_ge(s.g_ready, base + (r + 1))
                x = gate[:, r % UNITS, :]
                nc.gpsimd.tensor_tensor(x, x, m.xT[:, c * B + b, t0:t0 + N], ALU.mult).then_inc(s.gz_ready, 1)

            def remain(base, r):
                pool.wait_ge(s.j_ready, base + (r + 1))
                nc.gpsimd.tensor_tensor(rest[:, r % UNITS, :], slope[:, r % UNITS, :], before(r % BODY),
                                        ALU.mult).then_inc(s.jp_ready, 1)

            def body(base, r, first):
                if not first or r >= LAG_J:
                    remain(base, r - LAG_J)
                weigh(base, r)

            def tail(base):
                for r in range(UNITS):
                    if r < LAG_J:
                        remain(base, r - LAG_J)
                    weigh(base, r)
                for r in range(UNITS):
                    b, t0, c = unit(r)
                    pool.wait_ge(s.f_ready, base + (r + 1))
                    nc.gpsimd.tensor_tensor(rest[:, r, :], step[:, r, :], m.h[:, c * B + b, 1 + t0:1 + t0 + N],
                                            ALU.subtract).then_inc(s.diff_ready, 1)

            slots(pool, body, tail)

        @block.vector
        def _(dve):
            nc.vector.memset(zero[:], 0.0).then_inc(s.leaks, 1)
            dve.wait_ge(s.w_in, W_IN)
            nc.vector.tensor_scalar(leak[:], alpha[:], -1.0, 1.0, ALU.mult, ALU.add).then_inc(s.leaks, 1)
            dve.wait_ge(s.leaks, 2)
            nc.vector.tensor_scalar(leak_neg[:], leak[:], -1.0, None, ALU.mult).then_inc(s.leaks, 1)
            nc.vector.tensor_copy(leak_j[:].rearrange("p (c b) -> p c b", b=B),
                                  leak[:].unsqueeze(2).broadcast_to([P, C, B])).then_inc(s.leaks, 1)
            for x in state:
                nc.vector.tensor_copy(x[:, :, 0], start[:].rearrange("p c b -> p (c b)")).then_inc(s.leaks, 1)
            dve.wait_ge(s.leaks, 6)
            dve.wait_ge(s.zw_ready, UNITS)

            def argument(base, r):
                b, t0, c = unit(r)
                dve.wait_ge(s.gz_ready, base + (r + 1))
                x = gate[:, r % UNITS, :]
                nc.vector.scalar_tensor_tensor(x, before(r % BODY), leak[:, c:c + 1], x, ALU.mult,
                                               ALU.add).then_inc(s.u_ready, 1)

            def slopes(base, r):
                b, t0, c = unit(r)
                dve.wait_ge(s.sq_ready, base + (r + 1))
                x = slope[:, r % UNITS, :]
                nc.vector.tensor_scalar(x, x, leak_neg[:, c:c + 1], leak[:, c:c + 1], ALU.mult,
                                        ALU.add).then_inc(s.j_ready, 1)

            def subtract(base, r):
                dve.wait_ge(s.jp_ready, base + (r + 1))
                x = rest[:, r % UNITS, :]
                nc.vector.tensor_tensor(x, step[:, r % UNITS, :], x, ALU.subtract).then_inc(s.c_ready, 1)

            def solve(base, r):
                b, t0, c = unit(r)
                j = c * B + b
                to = state[(r // UNITS + 1) % 2]
                dve.wait_ge(s.c_ready, base + (r + 1))
                dve.wait_ge(s.h_ready, base + (r + UNITS - 1))
                nc.vector.tensor_tensor_scan(to[:, j, 1 + t0:1 + t0 + N], slope[:, r % UNITS, :], rest[:, r % UNITS, :],
                                             to[:, j, t0:t0 + 1], ALU.mult, ALU.add).then_inc(s.h_ready, 1)

            def body(base, r, first):
                if not first or r >= LAG_SCAN:
                    solve(base, r - LAG_SCAN)
                if not first or r >= LAG_REST:
                    subtract(base, r - LAG_REST)
                if not first or r >= LAG_U:
                    argument(base, r - LAG_U)
                if not first or r >= LAG_J:
                    slopes(base, r - LAG_J)

            def tail(base):
                for r in range(UNITS + LAG_U):
                    if r < LAG_SCAN:
                        solve(base, r - LAG_SCAN)
                    if r < LAG_REST:
                        subtract(base, r - LAG_REST)
                    argument(base, r - LAG_U)
                    if r < LAG_J:
                        slopes(base, r - LAG_J)
                for r in range(UNITS):
                    dve.wait_ge(s.diff_ready, r + 1)
                    nc.vector.tensor_reduce(worst[:, r:r + 1], rest[:, r, :], AX.X, ALU.max,
                                            apply_absolute_value=True).then_inc(s.worst_ready, 1)

            slots(dve, body, tail)
            dve.wait_ge(s.worst_ready, UNITS)
            nc.vector.tensor_scalar(fine[:], worst[:], TOL, None, ALU.is_le).then_inc(s.fine_ready, 1)
            dve.wait_ge(s.fine_psum, 1)
            nc.vector.tensor_reduce(found[:, 0:1], bank[0][:, 0:UNITS], AX.X, ALU.add).then_inc(s.verdict, 1)
            dve.wait_ge(s.verdict, 1)
            nc.vector.tensor_scalar(found[:, 1:2], found[:, 0:1], P * UNITS - 0.5, None, ALU.is_lt).then_inc(s.verdict, 1)
            dve.wait_ge(s.verdict, 2)
            nc.vector.tensor_copy(found_int[:], found[0:1, 1:2]).then_inc(s.verdict, 1)
            dve.wait_ge(s.verdict, 3)
            apart = dve.value_load(found_int[0:1, 0:1], min_val=0, max_val=1)
            with dve.If(apart > 0):
                nc.vector.tensor_copy(one[:, 0, :], m.h[:, :, 0]).then_inc(s.seq_h, 1)
                at = lambda x, t: x[:, :, bass.ds(t, 1)].rearrange("p j o -> p (j o)")
                with dve.Fori(0, T) as t:
                    dve.wait_ge(s.seq_h, t + 1)
                    nc.vector.tensor_tensor(one[:, 2, :], at(m.h, t), leak_j[:], ALU.mult).then_inc(s.seq_hl, 1)
                    dve.wait_ge(s.seq_psum, t + 1)
                    nc.vector.tensor_tensor(one[:, 0, :], bank[0][:, 0:J], at(zw, t), ALU.add).then_inc(s.seq_a, 1)
                    dve.wait_ge(s.seq_g, t + 1)
                    nc.vector.tensor_tensor(one[:, 1, :], one[:, 1, :], at(m.xT, t), ALU.mult).then_inc(s.seq_u, 1)
                    dve.wait_ge(s.seq_u, 2 * t + 1)
                    dve.wait_ge(s.seq_hl, t + 1)
                    nc.vector.tensor_tensor(one[:, 2, :], one[:, 2, :], one[:, 1, :], ALU.add).then_inc(s.seq_u, 1)
            dve.wait_ge(s.verdict, 3)


def experts(nc, d, m, out):
    TOK = B * T
    TILES = TOK // P
    K2 = EH // P
    with ExitStack() as own:
        sb = lambda n, s: own.enter_context(nc.sbuf_tensor("moe_" + n, s, F32))
        sem = lambda n: m.whole.enter_context(nc.semaphore("moe_" + n))
        I32 = mybir.dt.int32
        w2 = sb("w2", [P, E, K2, D])
        b1 = sb("b1", [P, E, K2])
        b2 = sb("b2", [P, E, D])
        gw = sb("gw", [P, C, E])
        gb = sb("gb", [P, E])
        order = sb("order", [P, E])
        before = sb("before", [P, P])
        edges = sb("edges", [P, TILES])
        ids = sb("ids", [P, BLOCKS])
        lg = sb("x_lg", [P, TILES, E])
        top = sb("x_top", [P, TILES])
        hot = sb("hot", [P, TILES, E])
        total = sb("total", [P, TILES, E])
        cum = sb("cum", [P, TILES + 1, E])
        more = sb("more", [P, E, TILES])
        nblk = sb("nblk", [P, E])
        first = sb("first", [P, E])
        place = sb("place", [P, TILES, E])
        slot = sb("slot", [P, TILES])
        slot_i = own.enter_context(nc.sbuf_tensor("slot_i", [P, TILES], I32))
        upto = sb("upto", [P, BLOCKS, E])
        eid = sb("eid", [P, BLOCKS])
        eid_i = own.enter_context(nc.sbuf_tensor("eid_i", [1, BLOCKS], I32))
        RING = 4
        row = sb("row", [P, RING, D])
        xin = sb("xin", [P, D])
        xt = sb("xt", [P, C, P])
        hid = sb("hid", [P, EH])
        ht = sb("ht", [P, K2, P])
        y = sb("y", [P, D])
        tr_bank = [own.enter_context(nc.psum_tensor(f"x_tr{i}", [P, N], F32)) for i in range(2)]
        hid_bank = [own.enter_context(nc.psum_tensor(f"x_hid{i}", [P, N], F32)) for i in range(2)]
        x_bank = own.enter_context(nc.psum_tensor("x_x", [P, D], F32))
        y_bank = own.enter_context(nc.psum_tensor("x_y", [P, D], F32))
        names = ("small_in", "w2_in", "b2_in", "lg_psum", "r", "count_psum", "slots_ready", "eid_ready", "turned",
                 "row_ready", "picked", "x_psum", "xt_ready", "hid_psum", "hid_ready", "ht_psum", "ht_ready",
                 "y_psum", "y_ready", "y_out", "z_psum", "sum_ready")
        s = namedtuple("ExpertSemaphores", names)(*(sem(n) for n in names))
        row_out = [sem(f"row_out{i}") for i in range(RING)]
        row_in = [sem(f"row_in{i}") for i in range(RING)]
        x_in, row_done = sem("x_in"), sem("row_done")
        SMALL = 7
        out_rows = out.rearrange("b t d -> (b t) d")
        block = own.enter_context(nc.Block())

        def tokens(x, a, c):
            b, t0 = divmod(a * P, T)
            off = x.shape[2] - T
            return x[:, c * B + b, off + t0:off + t0 + P]

        @block.sync
        def _(sp):
            sp.dma_start(gw[:], d.gate_wT.rearrange("(c p) e -> p c e", p=P)).then_inc(s.small_in, 16)
            sp.dma_start(gb[:], d.gate_b.partition_broadcast(P)).then_inc(s.small_in, 16)
            sp.dma_start(order[:], d.c_order).then_inc(s.small_in, 16)
            sp.dma_start(before[:], d.c_before).then_inc(s.small_in, 16)
            sp.dma_start(edges[:], d.c_edges).then_inc(s.small_in, 16)
            sp.dma_start(ids[:], d.c_ids).then_inc(s.small_in, 16)
            sp.dma_start(b1[:], d.b1).then_inc(s.small_in, 16)
            for e in range(E):
                sp.dma_start(w2[:, e], d.w2T[e].rearrange("(k p) n -> p k n", p=P)).then_inc(s.w2_in, 16)
            sp.dma_start(b2[:], d.b2.rearrange("e n -> (e n)").partition_broadcast(P)).then_inc(s.b2_in, 16)
            for i in range(RING):
                sp.wait_ge(row_out[i], 16 * (TILES // RING))
            sp.dma_start(xin[:], m.slots_in[0:P, :]).then_inc(x_in, 16)
            with sp.Fori(1, BLOCKS) as g:
                sp.wait_ge(s.x_psum, g)
                sp.dma_start(xin[:], m.slots_in[bass.ds(g * P, P), :]).then_inc(x_in, 16)
            for a in range(TILES):
                sp.wait_ge(s.sum_ready, a + 1)
                sp.dma_start(out_rows[a * P:(a + 1) * P, :], row[:, a % RING, :]).then_inc(row_done, 16)
            sp.wait_ge(row_done, 16 * TILES)

        @block.gpsimd
        def _(pool):
            pool.wait_ge(s.slots_ready, 1)
            for a in range(TILES):
                pool.wait_ge(s.row_ready, a + 1)
                nc.gpsimd.indirect_dma_start(
                    out=m.slots_in, out_offset=bass.IndirectOffsetOnAxis(ap=slot_i[:, a:a + 1], axis=0),
                    in_=row[:, a % RING, :], in_offset=None).then_inc(row_out[a % RING], 16)
            with pool.Fori(0, BLOCKS) as g:
                pool.wait_ge(s.y_ready, g + 1)
                nc.gpsimd.dma_start(m.slots_out[bass.ds(g * P, P), :], y[:]).then_inc(s.y_out, 16)
            pool.wait_ge(s.y_out, 16 * BLOCKS)
            for a in range(TILES):
                if a >= RING and a % RING == 0:
                    pool.wait_ge(row_done, 16 * a)
                nc.gpsimd.indirect_dma_start(
                    out=row[:, a % RING, :], out_offset=None, in_=m.slots_out,
                    in_offset=bass.IndirectOffsetOnAxis(ap=slot_i[:, a:a + 1], axis=0)).then_inc(row_in[a % RING], 16)

        @block.tensor
        def _(pe):
            pe.wait_ge(s.small_in, SMALL * 16)
            for a in range(TILES):
                for c in range(C):
                    last = nc.tensor.matmul(y_bank[:, a * E:(a + 1) * E], tokens(m.h, a, c), gw[:, c, :],
                                            start=(c == 0), stop=(c == C - 1))
            last.then_inc(s.lg_psum, 1)

            def turn(a):
                if a >= 2:
                    pe.wait_ge(s.row_ready, a - 1)
                for c in range(C):
                    last = nc.tensor.transpose(tr_bank[a % 2][:, c * P:(c + 1) * P], tokens(m.h, a, c), m.eye[:])
                last.then_inc(s.turned, 1)

            for a in range(RING):
                turn(a)
            pe.wait_ge(s.r, 4)
            flat = hot[:].rearrange("p a e -> p (a e)")
            nc.tensor.matmul(hid_bank[0][:, 0:TILES * E], before[:], flat, start=True, stop=True)
            nc.tensor.matmul(hid_bank[1][:, 0:TILES * E], m.ones[:], flat, start=True, stop=True).then_inc(s.count_psum, 1)
            for a in range(RING, TILES):
                turn(a)
            pe.wait_ge(s.row_ready, TILES)
            pe.wait_ge(s.eid_ready, 1)
            pe.wait_ge(s.w2_in, 16 * E)

            def turn_in(g):
                pe.wait_ge(x_in, g * 16 + 16)
                for c in range(C):
                    last = nc.tensor.transpose(x_bank[:, c * P:(c + 1) * P], xin[:, c * P:(c + 1) * P], m.eye[:])
                last.then_inc(s.x_psum, 1)

            def hidden(g, e):
                pe.wait_ge(s.xt_ready, g + 1)
                for n in range(EH // N):
                    for c in range(C):
                        last = nc.tensor.matmul(hid_bank[n][:], xt[:, c, :], m.w1[:, bass.ds(e, 1), c, n * N:(n + 1) * N].rearrange("p o n -> p (o n)"),
                                                start=(c == 0), stop=(c == C - 1))
                    last.then_inc(s.hid_psum, 1)

            def output(g, e):
                pe.wait_ge(s.ht_ready, g * K2 + K2)
                for k in range(K2):
                    last = nc.tensor.matmul(y_bank[:], ht[:, k, :],
                                            w2[:, bass.ds(e, 1), k, :].rearrange("p o n -> p (o n)"), start=(k == 0), stop=(k == K2 - 1))
                last.then_inc(s.y_psum, 1)

            def turn_hidden(g):
                for n in range(2):
                    pe.wait_ge(s.hid_ready, g * 2 + (n + 1))
                    for k in range(K2 // 2):
                        kk = n * (K2 // 2) + k
                        last = nc.tensor.transpose(tr_bank[n][:, k * P:(k + 1) * P], hid[:, kk * P:(kk + 1) * P], m.eye[:])
                    last.then_inc(s.ht_psum, 1)

            def expert(g):
                return pe.value_load(eid_i[0:1, bass.ds(g, 1)], min_val=0, max_val=E - 1)

            LAST = BLOCKS - 1
            turn_in(0)
            hidden(0, expert(0))
            turn_in(1)
            turn_hidden(0)
            hidden(1, expert(1))
            turn_in(2)
            output(0, expert(0))
            turn_hidden(1)
            with pe.Fori(2, LAST) as g:
                hidden(g, expert(g))
                turn_in(g + 1)
                pe.wait_ge(s.y_ready, g - 1)
                output(g - 1, expert(g - 1))
                turn_hidden(g)
            hidden(LAST, expert(LAST))
            pe.wait_ge(s.y_ready, LAST - 1)
            output(LAST - 1, expert(LAST - 1))
            turn_hidden(LAST)
            pe.wait_ge(s.y_ready, LAST)
            output(LAST, expert(LAST))
            for a in range(TILES):
                if a >= 2:
                    pe.wait_ge(s.sum_ready, a - 1)
                for c in range(C):
                    last = nc.tensor.transpose(hid_bank[a % 2][:, c * P:(c + 1) * P], tokens(m.xT, a, c), m.eye[:])
                last.then_inc(s.z_psum, 1)

        @block.scalar
        def _(act):
            for a in range(TILES):
                act.wait_ge(s.turned, a + 1)
                if a >= RING:
                    act.wait_ge(row_out[a % RING], 16 * (a // RING))
                nc.scalar.copy(row[:, a % RING, :], tr_bank[a % 2][:, 0:D]).then_inc(s.row_ready, 1)
            act.wait_ge(s.eid_ready, 1)
            with act.Fori(0, BLOCKS) as g:
                e = act.value_load(eid_i[0:1, bass.ds(g, 1)], min_val=0, max_val=E - 1)
                for k in range(K2):
                    act.wait_ge(s.ht_psum, g * 2 + (k // (K2 // 2) + 1))
                    nc.scalar.activation(ht[:, k, :], tr_bank[k // (K2 // 2)][:, k % (K2 // 2) * P:(k % (K2 // 2) + 1) * P],
                                         ACT.Relu, bias=b1[:, bass.ds(e, 1), k]).then_inc(s.ht_ready, 1)

        @block.vector
        def _(dve):
            def step(n, ins):
                ins.then_inc(s.r, 1)
                dve.wait_ge(s.r, n)

            wide = lambda x: x[:].unsqueeze(1).broadcast_to([P, TILES, E])
            dve.wait_ge(s.small_in, SMALL * 16)
            dve.wait_ge(s.lg_psum, 1)
            nc.vector.tensor_tensor(lg[:], y_bank[:, 0:TILES * E].rearrange("p (a e) -> p a e", e=E), wide(gb),
                                    ALU.add).then_inc(s.r, 1)
            dve.wait_ge(s.r, 1)
            nc.vector.tensor_reduce(top[:], lg[:], AX.X, ALU.max).then_inc(s.r, 1)
            dve.wait_ge(s.r, 2)
            nc.vector.tensor_tensor(lg[:], lg[:], top[:].unsqueeze(2).broadcast_to([P, TILES, E]),
                                    ALU.is_equal).then_inc(s.r, 1)
            dve.wait_ge(s.r, 3)
            nc.vector.tensor_tensor(lg[:], lg[:], wide(order), ALU.mult).then_inc(s.picked, 1)
            dve.wait_ge(s.picked, 1)
            nc.vector.tensor_reduce(top[:], lg[:], AX.X, ALU.max).then_inc(s.picked, 1)
            dve.wait_ge(s.picked, 2)
            nc.vector.tensor_tensor(hot[:], lg[:], top[:].unsqueeze(2).broadcast_to([P, TILES, E]),
                                    ALU.is_equal).then_inc(s.r, 1)
            dve.wait_ge(s.count_psum, 1)
            nc.vector.tensor_copy(total[:], hid_bank[1][:, 0:TILES * E].rearrange("p (a e) -> p a e", e=E)).then_inc(s.r, 1)
            nc.vector.memset(cum[:, 0, :], 0.0).then_inc(s.r, 1)
            for a in range(TILES):
                dve.wait_ge(s.r, 6 + a)
                nc.vector.tensor_tensor(cum[:, a + 1, :], cum[:, a, :], total[:, a, :], ALU.add).then_inc(s.r, 1)
            n = 6 + TILES
            dve.wait_ge(s.r, n)
            nc.vector.tensor_tensor(more[:], cum[:, TILES, :].unsqueeze(2).broadcast_to([P, E, TILES]),
                                    edges[:].unsqueeze(1).broadcast_to([P, E, TILES]), ALU.is_gt).then_inc(s.r, 1)
            dve.wait_ge(s.r, n + 1)
            nc.vector.tensor_reduce(nblk[:], more[:], AX.X, ALU.add).then_inc(s.r, 1)
            nc.vector.memset(first[:, 0:1], 0.0).then_inc(s.r, 1)
            for e in range(E - 1):
                dve.wait_ge(s.r, n + 3 + e)
                nc.vector.tensor_tensor(first[:, e + 1:e + 2], first[:, e:e + 1], nblk[:, e:e + 1], ALU.add).then_inc(s.r, 1)
            n += E + 2
            dve.wait_ge(s.r, n)
            nc.vector.scalar_tensor_tensor(place[:], wide(first), float(P), cum[:, 0:TILES, :], ALU.mult,
                                           ALU.add).then_inc(s.r, 1)
            dve.wait_ge(s.r, n + 1)
            nc.vector.tensor_tensor(place[:], place[:], hid_bank[0][:, 0:TILES * E].rearrange("p (a e) -> p a e", e=E),
                                    ALU.add).then_inc(s.r, 1)
            dve.wait_ge(s.r, n + 2)
            nc.vector.tensor_tensor(place[:], place[:], hot[:], ALU.mult).then_inc(s.r, 1)
            dve.wait_ge(s.r, n + 3)
            nc.vector.tensor_reduce(slot[:], place[:], AX.X, ALU.add).then_inc(s.r, 1)
            dve.wait_ge(s.r, n + 4)
            nc.vector.tensor_copy(slot_i[:], slot[:]).then_inc(s.slots_ready, 1)
            nc.vector.tensor_tensor(upto[:], first[:].unsqueeze(1).broadcast_to([P, BLOCKS, E]),
                                    ids[:].unsqueeze(2).broadcast_to([P, BLOCKS, E]), ALU.is_le).then_inc(s.r, 1)
            dve.wait_ge(s.r, n + 5)
            nc.vector.tensor_reduce(eid[:], upto[:], AX.X, ALU.add).then_inc(s.r, 1)
            dve.wait_ge(s.r, n + 6)
            nc.vector.tensor_scalar(eid[:], eid[:], -1.0, None, ALU.add).then_inc(s.r, 1)
            dve.wait_ge(s.r, n + 7)
            nc.vector.tensor_copy(eid_i[:], eid[0:1, :]).then_inc(s.eid_ready, 1)
            dve.wait_ge(s.eid_ready, 1)
            dve.wait_ge(s.b2_in, 16)

            def x_out(g):
                dve.wait_ge(s.x_psum, g + 1)
                nc.vector.tensor_copy(xt[:], x_bank[:].rearrange("p (c t) -> p c t", c=C)).then_inc(s.xt_ready, 1)

            def hid_out(g):
                for n in range(2):
                    dve.wait_ge(s.hid_psum, g * 2 + (n + 1))
                    nc.vector.tensor_copy(hid[:, n * N:(n + 1) * N], hid_bank[n][:]).then_inc(s.hid_ready, 1)

            def y_out(g, wait_store):
                e = dve.value_load(eid_i[0:1, bass.ds(g, 1)], min_val=0, max_val=E - 1)
                dve.wait_ge(s.y_psum, g + 1)
                if wait_store:
                    dve.wait_ge(s.y_out, g * 16)
                nc.vector.tensor_tensor(y[:], y_bank[:], b2[:, bass.ds(e, 1), :].rearrange("p o n -> p (o n)"),
                                        ALU.add).then_inc(s.y_ready, 1)

            x_out(0)
            hid_out(0)
            x_out(1)
            hid_out(1)
            x_out(2)
            y_out(0, False)
            with dve.Fori(2, BLOCKS - 1) as g:
                hid_out(g)
                x_out(g + 1)
                y_out(g - 1, True)
            hid_out(BLOCKS - 1)
            y_out(BLOCKS - 2, True)
            y_out(BLOCKS - 1, True)
            for a in range(TILES):
                dve.wait_ge(s.z_psum, a + 1)
                dve.wait_ge(row_in[a % RING], 16 * (a // RING + 1))
                nc.vector.tensor_tensor(row[:, a % RING, :], hid_bank[a % 2][:, 0:D], row[:, a % RING, :],
                                        ALU.add).then_inc(s.sum_ready, 1)


def constants():
    eye = np.eye(P, dtype=np.float32)
    i = np.arange(P)
    head_ones = (i[:, None] // DV == i[None, :] // DV).astype(np.float32)
    row, col = i[:, None], i[None, :]
    fill = [((row // (2 * b) == col // (2 * b)) & (row % (2 * b) >= b) & (col % (2 * b) < b)).astype(np.float32) + eye
            for b in (2 ** n for n in range(LEVELS))]
    masks = np.stack([*fill,
                      fill[0].T,
                      -(row < col).astype(np.float32),
                      (row <= col).astype(np.float32)], 1)
    pick = np.zeros((P, 2 * P), np.float32)
    pick[0:DV, P] = 1
    pick[DV:P, P + 32] = 1
    spread = np.zeros((48, 4 * C * B, P), np.float32)
    for g in range(4 * C * B):
        spread[g, g, 0:DV] = 1
        spread[32 + g, g, DV:P] = 1
    return {"c_eye": eye, "c_pick": pick, "c_spread": spread, "c_head_ones": head_ones, "c_masks": masks,
            "c_before": (row < col).astype(np.float32),
            "c_edges": np.tile(P * np.arange(B * T // P, dtype=np.float32), (P, 1)),
            "c_ids": np.tile(np.arange(BLOCKS, dtype=np.float32), (P, 1)),
            "c_order": np.tile(np.arange(E, 0, -1, dtype=np.float32), (P, 1))}


def layer_kernel(nc, ins, out):
    d = namedtuple("Inputs", ins)(**ins)
    with ExitStack() as ctx:
        def sb(name, shape, life=ctx):
            return life.enter_context(nc.sbuf_tensor(name, shape, F32))
        m = Shared()
        m.whole = ctx
        m.eye = sb("eye", [P, P])
        m.ones = sb("ones", [P, P])
        m.eps6 = sb("eps6", [P, 1])
        m.eps5 = sb("eps5", [P, 1])
        m.tiny = sb("tiny", [P, 1])
        m.xT = sb("xT", [P, J, T])
        consts_in = ctx.enter_context(nc.semaphore("consts_in"))
        with ExitStack() as attn:
            m.head_ones = sb("head_ones", [P, P], attn)
            m.w1s = sb("w1s", [P, HF], attn)
            m.hs = sb("hs", [P, J, T], attn)
            with nc.Block() as block:
                @block.sync
                def _(sp):
                    sp.dma_start(m.eye[:], d.c_eye).then_inc(consts_in, 16)
                    sp.dma_start(m.head_ones[:], d.c_head_ones).then_inc(consts_in, 16)
                    sp.wait_ge(consts_in, 32)

                @block.vector
                def _(dve):
                    nc.vector.memset(m.ones[:], 1.0)
                    nc.vector.memset(m.eps6[:], 1e-6)
                    nc.vector.memset(m.eps5[:], 1e-5)
                    nc.vector.memset(m.tiny[:], 1e-30)
            load_and_spike(nc, d, m)
            m.q = sb("q", [P, J, T], attn)
            m.v = sb("v", [P, J, FPAD + T], attn)
            m.fir_s, m.fir_m, m.fir_l = (sb(f"fir{i}", [P, J, T], attn) for i in range(3))
            with ExitStack() as delta:
                m.k = sb("k", [P, J, T], delta)
                m.beta = sb("beta", [P, J, T], delta)
                project(nc, d, m)
                attend(nc, d, m)
            mix(nc, d, m)
        m.h = sb("h", [P, J, 1 + T])
        m.w1 = sb("w1", [P, E, C, EH])
        m.slots_in = nc.dram_tensor("slots_in", (BLOCKS * P, D), F32).ap()
        m.slots_out = nc.dram_tensor("slots_out", (BLOCKS * P, D), F32).ap()
        recur(nc, d, m)
        experts(nc, d, m, out)


_ATTN = ["Wq", "Wk", "Wv", "conv_q", "conv_k", "conv_v", "Wb", "fir_s", "fir_m", "fir_l", "gW1", "gb1", "gW2",
         "gb2", "log_tau", "eps_logit", "norm_w", "Wo"]


def kernel(**inputs):
    import numpy as _np
    import concourse.bacc as _bacc
    from concourse import mybir as _mybir
    from concourse.bass_utils import run_bass_kernel_spmd as _run

    a = {k: _np.asarray(v) for k, v in inputs.items()}
    lay = {k: a["L0_attn_" + k] for k in _ATTN}
    lay["xT"] = a["x"].transpose(2, 0, 1)
    lay["condT"] = a["cond_1024"].T
    lay["wgT"] = a["L0_cond2_W"].T
    lay["bg"] = a["L0_cond2_b"].reshape(C, P).T
    lay["alpha"] = a["L0_cond2_alpha"].reshape(C, P).T
    lay["gate_wT"] = a["L0_ffn_gate_w"].T
    lay["gate_b"] = a["L0_ffn_gate_b"]
    lay["w1T"] = a["L0_ffn_w1"].transpose(0, 2, 1)
    lay["b1"] = a["L0_ffn_b1"].reshape(E, EH // P, P).transpose(2, 0, 1)
    lay["w2T"] = a["L0_ffn_w2"].transpose(0, 2, 1)
    lay["b2"] = a["L0_ffn_b2"]
    lay.update(constants())
    nc = _bacc.Bacc("TRN2", target_bir_lowering=False, num_devices=1)
    arrays, ins = {}, {}
    for name, v in lay.items():
        v = _np.ascontiguousarray(v)
        arrays[f"in_{name}"] = v
        ins[name] = nc.dram_tensor(f"in_{name}", v.shape, _mybir.dt.from_np(v.dtype), kind="ExternalInput").ap()
    out = nc.dram_tensor("out_0", (B, T, D), _mybir.dt.float32, kind="ExternalOutput").ap()
    layer_kernel(nc, ins, out)
    return _run(nc, [arrays], core_ids=[0]).results[0]["out_0"]
```
